# Optimizing a Trainium2 kernel written in Bass

```python
import numpy as np
import jax
import jax.numpy as jnp

def _softmax(x, axis=-1):
    return jax.nn.softmax(x, axis=axis)

def _gelu(x):
    return jax.nn.gelu(x, approximate=True)

def _silu(x):
    return jax.nn.silu(x)

def _sigmoid(x):
    return jax.nn.sigmoid(x)

def _layernorm(x, axis=-1, eps=1e-05):
    m = jnp.mean(x, axis=axis, keepdims=True)
    v = jnp.var(x, axis=axis, keepdims=True)
    return (x - m) / jnp.sqrt(v + eps)

def _scatter_add(tgt, idx, src, axis=0):
    return tgt.at[idx].add(src)

def _segment_sum(src, seg, n):
    return jax.ops.segment_sum(src, seg, n)
kernel_name = 'mk_cond_seq_d4_seqx_r8_7e983a'

def setup_inputs(seed: int=0):
    np.random.seed(seed)
    _w = jnp.asarray

    def _rec_inputs():
        import jax
        import jax.numpy as jnp
        _rk = jax.random.key(seed)
        x = -0.000125 + 0.9999 * jax.random.normal(jax.random.fold_in(_rk, 1), (32, 32, 128), jnp.float32)
        _lenS = 32 - jax.random.randint(jax.random.fold_in(_rk, 7), (32,), 0, max(1, 32 // 4) + 1, jnp.int32)
        _lenS2 = 32 - jax.random.randint(jax.random.fold_in(_rk, 8), (32,), 0, max(1, 32 // 4) + 1, jnp.int32)
        itok_B_0_15 = jax.random.randint(jax.random.fold_in(_rk, 11), (32,), 0, 16, jnp.int32)
        itok_B_34_63 = jax.random.randint(jax.random.fold_in(_rk, 13), (32,), 34, 64, jnp.int32)
        fside_Bx16xSxS_0 = -1.47943e-05 + 1.00017 * jax.random.normal(jax.random.fold_in(_rk, 14), (32, 16, 32, 32), jnp.float32)
        itok_B_0_7 = jax.random.randint(jax.random.fold_in(_rk, 15), (32,), 0, 8, jnp.int32)
        condB_gatescore = jax.random.uniform(jax.random.fold_in(_rk, 16), (32,), jnp.float32, 0.0, 0.581427)
        _validS = jnp.arange(32)[None, :] < _lenS[:, None]
        _validS2 = jnp.arange(32)[None, :] < _lenS2[:, None]
        _causal = jnp.tril(jnp.ones((32, 32), dtype=bool))
        mask_Bx1xSxS_bk0 = jnp.logical_not(jnp.broadcast_to(_validS[:, None, None, :], (32, 1, 32, 32)))
        return (x, itok_B_0_15, itok_B_34_63, fside_Bx16xSxS_0, itok_B_0_7, condB_gatescore, mask_Bx1xSxS_bk0)
    x, itok_B_0_15, itok_B_34_63, fside_Bx16xSxS_0, itok_B_0_7, condB_gatescore, mask_Bx1xSxS_bk0 = _rec_inputs()

    def _L0_cond_setup():
        import jax, jax.numpy as jnp
        import numpy as np
        B, S, D = (32, 128, 128)
        A = 32
        E = 16
        LN_EPS = 1e-05
        key = jax.random.key(seed)
        ks = jax.random.split(key, 10)
        s = lambda fan_in: 1.0 / np.sqrt(fan_in)
        return {'hidden_states': jax.random.normal(ks[0], (B, S, D), dtype=jnp.float32), 'domain_id': jax.random.randint(ks[1], (B,), 0, E, dtype=jnp.int64), 'down_W': jax.random.uniform(ks[2], (A, D), jnp.float32, -s(D), s(D)), 'down_b': jax.random.uniform(ks[3], (A,), jnp.float32, -s(D), s(D)), 'up_W': jax.random.uniform(ks[4], (D, A), jnp.float32, -s(A), s(A)), 'up_b': jax.random.uniform(ks[5], (D,), jnp.float32, -s(A), s(A)), 'expert_W': jax.random.uniform(ks[6], (E, A, A), jnp.float32, -s(A), s(A)), 'expert_b': jax.random.uniform(ks[7], (E, A), jnp.float32, -s(A), s(A)), 'domain_emb': jax.random.normal(ks[8], (E, A), dtype=jnp.float32), 'ln_gamma': jnp.ones((D,), jnp.float32), 'ln_beta': jnp.zeros((D,), jnp.float32)}
    _L0_cond_all = _L0_cond_setup()
    _L0_cond_in = {k: v for k, v in _L0_cond_all.items() if k in ('down_W', 'down_b', 'up_W', 'up_b', 'expert_W', 'expert_b', 'domain_emb', 'ln_gamma', 'ln_beta')}
    del _L0_cond_all

    def _L1_cond_setup():
        import jax, jax.numpy as jnp
        import numpy as np
        import math
        D_MODEL = 128
        N_HEAD = 16
        HEAD_DIM = D_MODEL // N_HEAD
        D_FF = 512
        NUM_STEPS = 100.0
        RESCALE = 4000.0
        EPS = 1e-05

        def _sin_emb(t):
            half = D_MODEL // 2
            x = t.astype(jnp.float32) / NUM_STEPS * RESCALE
            freqs = jnp.exp(jnp.arange(half, dtype=jnp.float32) * (-math.log(10000.0) / (half - 1)))
            e = x[:, None] * freqs[None, :]
            return jnp.concatenate([jnp.sin(e), jnp.cos(e)], axis=-1)

        def _ln(x):
            m = jnp.mean(x, axis=-1, keepdims=True)
            v = jnp.var(x, axis=-1, keepdims=True)
            return (x - m) / jnp.sqrt(v + EPS)

        def _gelu2(x):
            return x * jax.nn.sigmoid(1.702 * x)
        key = jax.random.key(seed)
        ks = jax.random.split(key, 24)
        B, S, D, F = (4, 64, D_MODEL, D_FF)
        std = 0.02
        inp = {'src': jax.random.normal(ks[0], (B, S, D), dtype=jnp.float32), 'src_mask': jax.random.randint(ks[1], (B, 1, S, S), 0, 2).astype(bool), 'timestep': jax.random.randint(ks[2], (B,), 0, 100, dtype=jnp.int32), 'attention_bias': jax.random.normal(ks[3], (B, N_HEAD, S, S), dtype=jnp.float32), 'W_ada': jax.random.normal(ks[4], (D, 2 * D), dtype=jnp.float32) * std, 'b_ada': jnp.zeros((2 * D,), dtype=jnp.float32), 'Wq': jax.random.normal(ks[5], (D, D), dtype=jnp.float32) * std, 'bq': jnp.zeros((D,), dtype=jnp.float32), 'Wk': jax.random.normal(ks[6], (D, D), dtype=jnp.float32) * std, 'bk': jnp.zeros((D,), dtype=jnp.float32), 'Wv': jax.random.normal(ks[7], (D, D), dtype=jnp.float32) * std, 'bv': jnp.zeros((D,), dtype=jnp.float32), 'Wo': jax.random.normal(ks[8], (D, D), dtype=jnp.float32) * std, 'bo': jnp.zeros((D,), dtype=jnp.float32), 'W1': jax.random.normal(ks[9], (D, F), dtype=jnp.float32) * std, 'b1': jnp.zeros((F,), dtype=jnp.float32), 'W2': jax.random.normal(ks[10], (F, D), dtype=jnp.float32) * std, 'b2': jnp.zeros((D,), dtype=jnp.float32), 'g2': jnp.ones((D,), dtype=jnp.float32), 'beta2': jnp.zeros((D,), dtype=jnp.float32)}
        return inp
    _L1_cond_all = _L1_cond_setup()
    _L1_cond_in = {k: v for k, v in _L1_cond_all.items() if k in ('W_ada', 'b_ada', 'Wq', 'bq', 'Wk', 'bk', 'Wv', 'bv', 'Wo', 'bo', 'W1', 'b1', 'W2', 'b2', 'g2', 'beta2')}
    del _L1_cond_all

    def _L2_cond_setup():
        import jax, jax.numpy as jnp
        import numpy as np
        E, H, I = (8, 128, 512)
        B, S = (4, 128)
        LN_EPS = 1e-12
        key = jax.random.key(seed)
        ks = jax.random.split(key, 8)
        x = jax.random.normal(ks[0], (B, S, H), dtype=jnp.float32)
        expert_idx = jax.random.randint(ks[1], (B,), 0, E, dtype=jnp.int64)
        Wi = jax.random.normal(ks[2], (E, H, I), dtype=jnp.float32) * 0.02
        bi = jnp.zeros((E, I), dtype=jnp.float32)
        Wo = jax.random.normal(ks[3], (E, I, H), dtype=jnp.float32) * 0.02
        bo = jnp.zeros((E, H), dtype=jnp.float32)
        gamma = jnp.ones((E, H), dtype=jnp.float32)
        beta = jnp.zeros((E, H), dtype=jnp.float32)
        return {'input_tensor': x, 'expert_idx': expert_idx, 'Wi': Wi, 'bi': bi, 'Wo': Wo, 'bo': bo, 'gamma': gamma, 'beta': beta}
    _L2_cond_all = _L2_cond_setup()
    _L2_cond_in = {k: v for k, v in _L2_cond_all.items() if k in ('Wi', 'bi', 'Wo', 'bo', 'gamma', 'beta')}
    del _L2_cond_all

    def _L3_cond_setup():
        import jax, jax.numpy as jnp
        import numpy as np
        D_MODEL = 128
        N_HEADS = 16
        D_HEAD = D_MODEL // N_HEADS
        D_FF = 512
        EPS = 1e-05

        def layernorm(x, gamma, beta):
            mu = jnp.mean(x, axis=-1, keepdims=True)
            var = jnp.var(x, axis=-1, keepdims=True)
            return (x - mu) * jax.lax.rsqrt(var + EPS) * gamma + beta
        key = jax.random.key(seed)
        ks = jax.random.split(key, 16)
        B, T = (4, 256)
        s = 1.0 / np.sqrt(D_MODEL)
        sf = 1.0 / np.sqrt(D_FF)
        return {'x': jax.random.normal(ks[0], (B, T, D_MODEL), jnp.float32), 'gate_score': jax.random.uniform(ks[1], (B,), jnp.float32), 'Wq': jax.random.normal(ks[2], (D_MODEL, D_MODEL), jnp.float32) * s, 'bq': jnp.zeros((D_MODEL,), jnp.float32), 'Wk': jax.random.normal(ks[3], (D_MODEL, D_MODEL), jnp.float32) * s, 'bk': jnp.zeros((D_MODEL,), jnp.float32), 'Wv': jax.random.normal(ks[4], (D_MODEL, D_MODEL), jnp.float32) * s, 'bv': jnp.zeros((D_MODEL,), jnp.float32), 'Wo': jax.random.normal(ks[5], (D_MODEL, D_MODEL), jnp.float32) * s, 'bo': jnp.zeros((D_MODEL,), jnp.float32), 'W1': jax.random.normal(ks[6], (D_MODEL, D_FF), jnp.float32) * s, 'b1': jnp.zeros((D_FF,), jnp.float32), 'W2': jax.random.normal(ks[7], (D_FF, D_MODEL), jnp.float32) * sf, 'b2': jnp.zeros((D_MODEL,), jnp.float32), 'gamma1': jnp.ones((D_MODEL,), jnp.float32), 'beta1': jnp.zeros((D_MODEL,), jnp.float32), 'gamma2': jnp.ones((D_MODEL,), jnp.float32), 'beta2': jnp.zeros((D_MODEL,), jnp.float32)}
    _L3_cond_all = _L3_cond_setup()
    _L3_cond_in = {k: v for k, v in _L3_cond_all.items() if k in ('Wq', 'bq', 'Wk', 'bk', 'Wv', 'bv', 'Wo', 'bo', 'W1', 'b1', 'W2', 'b2', 'gamma1', 'beta1', 'gamma2', 'beta2')}
    del _L3_cond_all
    return {'x': x, 'itok_B_0_15': itok_B_0_15, 'itok_B_34_63': itok_B_34_63, 'fside_Bx16xSxS_0': fside_Bx16xSxS_0, 'itok_B_0_7': itok_B_0_7, 'condB_gatescore': condB_gatescore, 'mask_Bx1xSxS_bk0': mask_Bx1xSxS_bk0, 'L0_cond_down_W': _L0_cond_in['down_W'], 'L0_cond_down_b': _L0_cond_in['down_b'], 'L0_cond_up_W': _L0_cond_in['up_W'], 'L0_cond_up_b': _L0_cond_in['up_b'], 'L0_cond_expert_W': _L0_cond_in['expert_W'], 'L0_cond_expert_b': _L0_cond_in['expert_b'], 'L0_cond_domain_emb': _L0_cond_in['domain_emb'], 'L0_cond_ln_gamma': _L0_cond_in['ln_gamma'], 'L0_cond_ln_beta': _L0_cond_in['ln_beta'], 'L1_cond_W_ada': _L1_cond_in['W_ada'], 'L1_cond_b_ada': _L1_cond_in['b_ada'], 'L1_cond_Wq': _L1_cond_in['Wq'], 'L1_cond_bq': _L1_cond_in['bq'], 'L1_cond_Wk': _L1_cond_in['Wk'], 'L1_cond_bk': _L1_cond_in['bk'], 'L1_cond_Wv': _L1_cond_in['Wv'], 'L1_cond_bv': _L1_cond_in['bv'], 'L1_cond_Wo': _L1_cond_in['Wo'], 'L1_cond_bo': _L1_cond_in['bo'], 'L1_cond_W1': _L1_cond_in['W1'], 'L1_cond_b1': _L1_cond_in['b1'], 'L1_cond_W2': _L1_cond_in['W2'], 'L1_cond_b2': _L1_cond_in['b2'], 'L1_cond_g2': _L1_cond_in['g2'], 'L1_cond_beta2': _L1_cond_in['beta2'], 'L2_cond_Wi': _L2_cond_in['Wi'], 'L2_cond_bi': _L2_cond_in['bi'], 'L2_cond_Wo': _L2_cond_in['Wo'], 'L2_cond_bo': _L2_cond_in['bo'], 'L2_cond_gamma': _L2_cond_in['gamma'], 'L2_cond_beta': _L2_cond_in['beta'], 'L3_cond_Wq': _L3_cond_in['Wq'], 'L3_cond_bq': _L3_cond_in['bq'], 'L3_cond_Wk': _L3_cond_in['Wk'], 'L3_cond_bk': _L3_cond_in['bk'], 'L3_cond_Wv': _L3_cond_in['Wv'], 'L3_cond_bv': _L3_cond_in['bv'], 'L3_cond_Wo': _L3_cond_in['Wo'], 'L3_cond_bo': _L3_cond_in['bo'], 'L3_cond_W1': _L3_cond_in['W1'], 'L3_cond_b1': _L3_cond_in['b1'], 'L3_cond_W2': _L3_cond_in['W2'], 'L3_cond_b2': _L3_cond_in['b2'], 'L3_cond_gamma1': _L3_cond_in['gamma1'], 'L3_cond_beta1': _L3_cond_in['beta1'], 'L3_cond_gamma2': _L3_cond_in['gamma2'], 'L3_cond_beta2': _L3_cond_in['beta2']}

def reference(x, itok_B_0_15, itok_B_34_63, fside_Bx16xSxS_0, itok_B_0_7, condB_gatescore, mask_Bx1xSxS_bk0, L0_cond_down_W, L0_cond_down_b, L0_cond_up_W, L0_cond_up_b, L0_cond_expert_W, L0_cond_expert_b, L0_cond_domain_emb, L0_cond_ln_gamma, L0_cond_ln_beta, L1_cond_W_ada, L1_cond_b_ada, L1_cond_Wq, L1_cond_bq, L1_cond_Wk, L1_cond_bk, L1_cond_Wv, L1_cond_bv, L1_cond_Wo, L1_cond_bo, L1_cond_W1, L1_cond_b1, L1_cond_W2, L1_cond_b2, L1_cond_g2, L1_cond_beta2, L2_cond_Wi, L2_cond_bi, L2_cond_Wo, L2_cond_bo, L2_cond_gamma, L2_cond_beta, L3_cond_Wq, L3_cond_bq, L3_cond_Wk, L3_cond_bk, L3_cond_Wv, L3_cond_bv, L3_cond_Wo, L3_cond_bo, L3_cond_W1, L3_cond_b1, L3_cond_W2, L3_cond_b2, L3_cond_gamma1, L3_cond_beta1, L3_cond_gamma2, L3_cond_beta2):
    import jax
    import jax.numpy as jnp

    def _L0_cond_ref(hidden_states, domain_id, down_W, down_b, up_W, up_b, expert_W, expert_b, domain_emb, ln_gamma, ln_beta):
        import jax, jax.numpy as jnp
        import numpy as np
        B, S, D = (32, 128, 128)
        A = 32
        E = 16
        LN_EPS = 1e-05
        residual = hidden_states
        hidden = jnp.einsum('bsd,ad->bsa', hidden_states, down_W) + down_b
        hidden = jax.nn.gelu(hidden, approximate=False)
        valid = (domain_id >= 0) & (domain_id < E)
        idx = jnp.clip(domain_id, 0, E - 1)
        Wsel = expert_W[idx]
        bsel = expert_b[idx]
        expert_out = jnp.einsum('bsa,boa->bso', hidden, Wsel) + bsel[:, None, :]
        domain_output = jnp.where(valid[:, None, None], expert_out, hidden)
        hidden = domain_output + domain_emb[idx][:, None, :]
        hidden = jnp.einsum('bsa,da->bsd', hidden, up_W) + up_b
        x = hidden + residual
        mu = jnp.mean(x, axis=-1, keepdims=True)
        var = jnp.mean(jnp.square(x - mu), axis=-1, keepdims=True)
        return (x - mu) * jax.lax.rsqrt(var + LN_EPS) * ln_gamma + ln_beta

    def _L1_cond_ref(src, src_mask, timestep, attention_bias, W_ada, b_ada, Wq, bq, Wk, bk, Wv, bv, Wo, bo, W1, b1, W2, b2, g2, beta2):
        import jax, jax.numpy as jnp
        import numpy as np
        import math
        D_MODEL = 128
        N_HEAD = 16
        HEAD_DIM = D_MODEL // N_HEAD
        D_FF = 512
        NUM_STEPS = 100.0
        RESCALE = 4000.0
        EPS = 1e-05

        def _sin_emb(t):
            half = D_MODEL // 2
            x = t.astype(jnp.float32) / NUM_STEPS * RESCALE
            freqs = jnp.exp(jnp.arange(half, dtype=jnp.float32) * (-math.log(10000.0) / (half - 1)))
            e = x[:, None] * freqs[None, :]
            return jnp.concatenate([jnp.sin(e), jnp.cos(e)], axis=-1)

        def _ln(x):
            m = jnp.mean(x, axis=-1, keepdims=True)
            v = jnp.var(x, axis=-1, keepdims=True)
            return (x - m) / jnp.sqrt(v + EPS)

        def _gelu2(x):
            return x * jax.nn.sigmoid(1.702 * x)
        B, S, D = src.shape
        emb = jax.nn.silu(_sin_emb(timestep)) @ W_ada + b_ada
        scale, shift = jnp.split(emb[:, None, :], 2, axis=-1)
        x = _ln(src) * (1.0 + scale) + shift
        q = (x @ Wq + bq).reshape(B, S, N_HEAD, HEAD_DIM).transpose(0, 2, 1, 3)
        k = (x @ Wk + bk).reshape(B, S, N_HEAD, HEAD_DIM).transpose(0, 2, 1, 3)
        v = (x @ Wv + bv).reshape(B, S, N_HEAD, HEAD_DIM).transpose(0, 2, 1, 3)
        scores = jnp.einsum('bhqd,bhkd->bhqk', q / math.sqrt(HEAD_DIM), k)
        scores = scores + attention_bias
        scores = jnp.where(src_mask, -jnp.inf, scores.astype(jnp.float32))
        probs = jax.nn.softmax(scores, axis=-1).astype(v.dtype)
        ctx = jnp.einsum('bhqk,bhkd->bhqd', probs, v)
        ctx = ctx.transpose(0, 2, 1, 3).reshape(B, S, D)
        x = x + (ctx @ Wo + bo)
        h = _ln(x) * g2 + beta2
        ff = _gelu2(h @ W1 + b1) @ W2 + b2
        return x + ff

    def _L2_cond_ref(input_tensor, expert_idx, Wi, bi, Wo, bo, gamma, beta):
        import jax, jax.numpy as jnp
        import numpy as np
        E, H, I = (8, 128, 512)
        B, S = (4, 128)
        LN_EPS = 1e-12
        Wi_b = Wi[expert_idx]
        bi_b = bi[expert_idx]
        Wo_b = Wo[expert_idx]
        bo_b = bo[expert_idx]
        g_b = gamma[expert_idx]
        be_b = beta[expert_idx]
        h = jax.nn.gelu(jnp.einsum('bsh,bhi->bsi', input_tensor, Wi_b) + bi_b[:, None, :], approximate=False)
        o = jnp.einsum('bsi,bih->bsh', h, Wo_b) + bo_b[:, None, :]
        r = o + input_tensor
        mu = jnp.mean(r, axis=-1, keepdims=True)
        var = jnp.mean(jnp.square(r - mu), axis=-1, keepdims=True)
        y = (r - mu) * jax.lax.rsqrt(var + LN_EPS)
        return y * g_b[:, None, :] + be_b[:, None, :]

    def _L3_cond_ref(x, gate_score, Wq, bq, Wk, bk, Wv, bv, Wo, bo, W1, b1, W2, b2, gamma1, beta1, gamma2, beta2):
        import jax, jax.numpy as jnp
        import numpy as np
        D_MODEL = 128
        N_HEADS = 16
        D_HEAD = D_MODEL // N_HEADS
        D_FF = 512
        EPS = 1e-05

        def layernorm(x, gamma, beta):
            mu = jnp.mean(x, axis=-1, keepdims=True)
            var = jnp.var(x, axis=-1, keepdims=True)
            return (x - mu) * jax.lax.rsqrt(var + EPS) * gamma + beta
        B, T, C = x.shape
        h = layernorm(x, gamma1, beta1)
        Q = (h @ Wq + bq).reshape(B, T, N_HEADS, D_HEAD).transpose(0, 2, 1, 3)
        K = (h @ Wk + bk).reshape(B, T, N_HEADS, D_HEAD).transpose(0, 2, 1, 3)
        V = (h @ Wv + bv).reshape(B, T, N_HEADS, D_HEAD).transpose(0, 2, 1, 3)
        scores = jnp.einsum('bhqd,bhkd->bhqk', Q, K) / np.sqrt(D_HEAD)
        causal = jnp.tril(jnp.ones((T, T), dtype=bool))
        scores = jnp.where(causal, scores, -jnp.inf)
        attn = jax.nn.softmax(scores, axis=-1)
        ctx = jnp.einsum('bhqk,bhkd->bhqd', attn, V)
        ctx = ctx.transpose(0, 2, 1, 3).reshape(B, T, C)
        attn_out = ctx @ Wo + bo
        x1 = x + attn_out
        h2 = layernorm(x1, gamma2, beta2)
        ff = jax.nn.gelu(h2 @ W1 + b1, approximate=False) @ W2 + b2
        x2 = x1 + ff
        g = gate_score[:, None, None]
        return x + g * (x2 - x)
    x = _L0_cond_ref(x, itok_B_0_15, L0_cond_down_W, L0_cond_down_b, L0_cond_up_W, L0_cond_up_b, L0_cond_expert_W, L0_cond_expert_b, L0_cond_domain_emb, L0_cond_ln_gamma, L0_cond_ln_beta)
    x = _L1_cond_ref(x, mask_Bx1xSxS_bk0, itok_B_34_63, fside_Bx16xSxS_0, L1_cond_W_ada, L1_cond_b_ada, L1_cond_Wq, L1_cond_bq, L1_cond_Wk, L1_cond_bk, L1_cond_Wv, L1_cond_bv, L1_cond_Wo, L1_cond_bo, L1_cond_W1, L1_cond_b1, L1_cond_W2, L1_cond_b2, L1_cond_g2, L1_cond_beta2)
    x = _L2_cond_ref(x, itok_B_0_7, L2_cond_Wi, L2_cond_bi, L2_cond_Wo, L2_cond_bo, L2_cond_gamma, L2_cond_beta)
    x = _L3_cond_ref(x, condB_gatescore, L3_cond_Wq, L3_cond_bq, L3_cond_Wk, L3_cond_bk, L3_cond_Wv, L3_cond_bv, L3_cond_Wo, L3_cond_bo, L3_cond_W1, L3_cond_b1, L3_cond_W2, L3_cond_b2, L3_cond_gamma1, L3_cond_beta1, L3_cond_gamma2, L3_cond_beta2)
    return x

_drawn_inputs = setup_inputs


def setup_inputs(seed=0):
    import zlib

    import numpy as np

    out = dict(_drawn_inputs(seed))
    spreads = {'L0_cond_ln_gamma': (1.0, 0.2),
     'L0_cond_ln_beta': (0.0, 0.1),
     'L1_cond_b_ada': (0.0, 0.1),
     'L1_cond_bq': (0.0, 0.8),
     'L1_cond_bk': (0.0, 0.8),
     'L1_cond_bv': (0.0, 0.351),
     'L1_cond_bo': (0.0, 0.1),
     'L1_cond_b1': (0.0, 0.369),
     'L1_cond_b2': (0.0, 0.1),
     'L1_cond_g2': (1.0, 0.6),
     'L1_cond_beta2': (0.0, 0.8),
     'L2_cond_bi': (0.0, 0.336),
     'L2_cond_bo': (0.0, 0.1),
     'L2_cond_gamma': (1.0, 0.2),
     'L2_cond_beta': (0.0, 0.1),
     'L3_cond_bq': (0.0, 0.8),
     'L3_cond_bk': (0.0, 0.8),
     'L3_cond_bv': (0.0, 0.1),
     'L3_cond_bo': (0.0, 0.1),
     'L3_cond_b1': (0.0, 0.357),
     'L3_cond_b2': (0.0, 0.1),
     'L3_cond_gamma1': (1.0, 0.2),
     'L3_cond_beta1': (0.0, 0.1),
     'L3_cond_gamma2': (1.0, 0.2),
     'L3_cond_beta2': (0.0, 0.344)}
    factors = {'fside_Bx16xSxS_0': 6.185, 'L0_cond_down_b': 5.879, 'L1_cond_Wq': 8.0, 'L1_cond_Wk': 8.0}
    for name, (base, spread) in spreads.items():
        noise = np.random.default_rng([zlib.crc32(name.encode()), seed]).standard_normal(out[name].shape)
        drawn = base * np.exp(spread * noise) if base else spread * noise
        out[name] = jnp.asarray(drawn.astype(out[name].dtype))
    for name, factor in factors.items():
        out[name] = (out[name] * factor).astype(out[name].dtype)
    return out
```

```python
import math
from contextlib import ExitStack

import concourse.bass as bass
from concourse import mybir

F32 = mybir.dt.float32
I32 = mybir.dt.int32
U8 = mybir.dt.uint8
ALU = mybir.AluOpType
ACT = mybir.ActivationFunctionType
AX = mybir.AxisListType

P = 128
B, S, D = 32, 32, 128
NB = P // S
NT = B // NB
H, DH = 16, 8
HG = 4
H4 = H // HG
A = 32
E0, E2 = 16, 8
FF = 512
C = FF // P
VW = H4 * DH + H4
SLOTS = 4
WSLOTS = 4
EPS = 1e-5
EPS2 = 1e-12
NEG = -1e30
TWO_PI = 2 * math.pi
PI_A = 6.28125
PI_B = 0.00193500518798828125
PI_C = TWO_PI - PI_A - PI_B
ROUND = 1.5 * 2.0**23

COLS = [
    ("ident", P), ("down_wt", A), ("seq_mask", NB), ("head_mask", H4), ("cvec", 32),
    ("w_ada", 2 * D), ("causal", S),
    ("wqk1", 2 * D), ("wv1", D), ("wo1", D), ("w11", FF), ("w21", FF),
    ("wqk3", 2 * D), ("wv3", D), ("wo3", D), ("w13", FF), ("w23", FF),
]
COL = {}
_at = 0
for _n, _w in COLS:
    COL[_n] = (_at, _w)
    _at += _w
NCOL = _at
(C_DOWN_B, C_FREQ, C_PHASE, C_IOTA, C_BV1, C_G2, C_BETA2, C_BV3, C_G31, C_B31, C_G32, C_B32) = range(12)
C_B1_1, C_B1_3 = 12, 16
ROWS = ["g0", "be0", "bqk1", "bk1", "bo1", "b21", "bqk3", "bk3", "bo3", "b23"]
ROW = {n: i * D for i, n in enumerate(ROWS)}
NROW = len(ROWS) * D

STEPS = """
down:pe gelu0:act expert:pe expert_bias:dve up:pe res0:dve
stat_a:dve rstd_a:act norm_a:dve aff_a:pool
stat_b:dve rstd_b:act norm_b:dve ada:pe aff_b:dve
tr_b:pe ev_b:act xbo1:pool
xr1:act qk1:pe qkb1:dve qkt1:dve qbd1:pool kex1:dve v1:pe vbd1:dve sc1:pe sb1:dve mx1:dve sub1:pool exp1:act
pt1:pe evpt1:act ctx1:pe cn1:dve ct1:pe evct1:act wo1:pe res1:dve
stat_c:dve xb21:pool rstd_c:act norm_c:dve tr_c:pe ev_c:act
ff1:pe act1:act fo1:pe res2:dve
tr_d:pe ev_d:act sel:pe evsel:act e1:pe eve1:act xbo2:pool et:pe eb:dve gelu2:act e2:pe res3:dve
stat_e:dve rstd_e:act norm_e:dve aff_e:pool
stat_f:dve rstd_f:act norm_f:dve tr_f:pe ev_f:act xbo3:pool
xr3:act qk3:pe qkb3:dve qkt3:dve qbd3:pool kex3:dve v3:pe vbd3:dve sc3:pe sb3:dve mx3:dve sub3:pool exp3:act
pt3:pe evpt3:act ctx3:pe cn3:dve ct3:pe evct3:act wo3:pe res4:dve
stat_g:dve xb23:pool rstd_g:act norm_g:dve tr_g:pe ev_g:act
ff3:pe act3:act fo3:pe res5:dve gate:dve store:sp
""".split()
STEPS = [tuple(s.split(":")) for s in STEPS]
LAG = 1.0
GROUP_LAG = 16.0


def order():
    keyed = []
    for i, (name, engine) in enumerate(STEPS):
        for t in range(NT):
            keyed.append((i + LAG * t + GROUP_LAG * (t // SLOTS), t, name, engine))
    return [(name, engine, t) for _, t, name, engine in sorted(keyed, key=lambda k: (k[0], k[1]))]


ORDER = order()

BANK = {
    "down": (0, "gelu0"), "expert": (1, "expert_bias"), "up": (2, "res0"),
    "ada": (1, "aff_b"), "tr_b": (0, "ev_b"),
    "sel": (1, "evsel"), "e1": (3, "eve1"), "et": (5, "eb"), "e2": (6, "res3"), "tr_d": (0, "ev_d"),
    "tr_c": (0, "ev_c"), "tr_f": (0, "ev_f"), "tr_g": (0, "ev_g"),
}
for _l, _r in (("1", "res1"), ("3", "res4")):
    BANK.update({
        "qk" + _l: (1, "qkb" + _l), "v" + _l: (3, "vbd" + _l), "sc" + _l: (4, "sb" + _l),
        "pt" + _l: (5, "evpt" + _l), "ctx" + _l: (6, "cn" + _l), "ct" + _l: (0, "evct" + _l),
        "wo" + _l: (2, _r), "ff" + _l: (7, "act" + _l),
    })
BANK["fo1"] = (6, "res2")
BANK["fo3"] = (6, "res5")


SLOT_USES = {
    "qk": [("qkb1", ["qkt1"]), ("qkb3", ["qkt3"])],
    "qkt": [("qkt1", ["qbd1", "kex1"]), ("qkt3", ["qbd3", "kex3"])],
    "qbd": [("qbd1", ["sc1"]), ("qbd3", ["sc3"])],
    "kex": [("kex1", ["sc1"]), ("kex3", ["sc3"])],
    "vbd": [("vbd1", ["ctx1"]), ("vbd3", ["ctx3"])],
    "sc": [("xr1", ["pt1"]), ("xr3", ["pt3"])],
    "pt": [("evpt1", ["ctx1"]), ("eve1", ["et"]), ("evpt3", ["ctx3"])],
    "cx": [("cn1", ["ct1"]), ("cn3", ["ct3"])],
    "cxt": [("evct1", ["wo1"]), ("evct3", ["wo3"])],
    "hg": [("act1", ["fo1"]), ("eb", ["e2"]), ("act3", ["fo3"])],
    "selv": [("evsel", ["aff_e"])],
}


def previous_use():
    starts = {name: (bank, [reader]) for name, (bank, reader) in BANK.items()}
    for buf, uses in SLOT_USES.items():
        for writer, readers in uses:
            starts[writer] = (buf, readers)
    at = {(name, t): i for i, (name, _, t) in enumerate(ORDER)}
    last, out = {}, {}
    for name, _, t in ORDER:
        if name in starts:
            what, readers = starts[name]
            if isinstance(what, str):
                what = (what, t % SLOTS)
            out[name, t] = last.get(what, ([], 0))
            for r in out[name, t][0]:
                assert isinstance(what, int) or at[r, out[name, t][1]] < at[name, t], (name, t, out[name, t])
            last[what] = (readers, t)
    return out


PREVIOUS = previous_use()


def build(nc, a, out):
    ctx = ExitStack()
    with ctx:
        def sb(name, shape, dt=F32):
            return ctx.enter_context(nc.sbuf_tensor(name, shape, dt))

        def sem(name):
            return ctx.enter_context(nc.semaphore(name))

        bank = [ctx.enter_context(nc.psum_tensor(f"bank{i}", [P, 512], F32)) for i in range(8)]

        tab = sb("tab", [P, NCOL])
        rows = sb("rows", [P, NROW])
        up33 = sb("up33", [A + 1, D])
        experts0 = sb("experts0", [E0 + 1, A * A])
        evec0 = sb("evec0", [E0 + 1, 2 * A])
        ada_b = sb("ada_b", [B, 2 * D])
        rep = sb("rep", [B, NT * P])
        evec2 = sb("evec2", [E2, FF + 3 * D])
        idx0 = sb("idx0", [E0 + 1, B], I32)
        idx1 = sb("idx1", [P, B], I32)
        idx2 = sb("idx2", [E2, B], I32)
        gate = sb("gate", [P, NT])
        mask_u8 = sb("mask_u8", [P, NT * S], U8)
        mask_add = sb("mask_add", [P, NT, S])

        def col(name, lo=0, n=None):
            at, w = COL[name]
            return tab[:, at + lo:at + lo + (w if n is None else n)]

        def cvec(i, parts=P):
            at = COL["cvec"][0] + i
            return tab[0:parts, at:at + 1]

        def row(name, n=D):
            return rows[:, ROW[name]:ROW[name] + n]

        ident = col("ident")

        f0 = sb("f0", [E0 + 1, 4, B])
        oh0 = sb("oh0", [E0 + 1, 2, B])
        wsel = sb("wsel", [A, A, B])
        bias0 = sb("bias0", [A, B])
        ang = sb("ang", [P, 4, B])
        silu_t = sb("silu_t", [P, B])
        emb = sb("emb", [B, 2 * D])
        f2 = sb("f2", [E2, 4, B])
        eidx = sb("eidx", [1, B], I32)
        oh2 = sb("oh2", [E2, B, S])
        bi_sel = sb("bi_sel", [P, C, B])
        eps = sb("eps", [P, 2])

        x_in = sb("x_in", [P, NT, D])
        res = sb("res", [P, NT, D])
        resb = sb("resb", [P, NT, D])
        nrm = sb("nrm", [P, NT, D])
        hid = nrm[0:A]
        hid2 = resb[0:A + 1]
        xt = sb("xt", [P, NT, P])
        fm = sb("fm", [P, SLOTS, H, S])
        bn = sb("bn", [P, NT, 6])
        mv = sb("mv", [P, NT, 2])
        lnv = sb("lnv", [P, NT])
        rstd = sb("rstd", [P, NT])
        mx = sb("mx", [P, NT, H])
        rsum = sb("rsum", [P, NT, H])
        selv = sb("selv", [P, SLOTS, 3 * D])
        qk = sb("qk", [P, SLOTS, 2 * D])
        qkt = sb("qkt", [P, SLOTS, 2, HG, S])
        qbd = sb("qbd", [P, SLOTS, HG, NB, S])
        kex = sb("kex", [P, SLOTS, HG, H4, S])
        vbd = sb("vbd", [P, SLOTS, NB, HG, VW])
        sc = sb("sc", [P, SLOTS, H, S])
        xr = sc[:].rearrange("p k (b r) s -> p k b (r s)", b=NB)
        pt = sb("pt", [P, SLOTS, HG, P])
        cx = sb("cx", [P, SLOTS, D])
        cxt = sb("cxt", [P, SLOTS, P])
        hg = sb("hg", [P, SLOTS, C, P])
        wexp = sb("wexp", [P, WSLOTS, NB, 2 * FF])

        done = {name: sem("done_" + name) for name, _ in STEPS}
        loaded = {n: sem("loaded_" + n) for n in
                  ("xt", "x", "tab0", "tab1", "tab3", "rows", "small0", "small1", "idx2", "evec2", "gate", "mask")}
        s_fs = [sem(f"fside_in{t}") for t in range(NT)]
        s_we = [sem(f"wexp_in{t}") for t in range(NT)]
        eidx_ready = sem("eidx_ready")
        oh0_ready = sem("oh0_ready")
        oh2_ready = sem("oh2_ready")
        angle_ready = sem("angle_ready")
        silu_ready = sem("silu_ready")
        wsel_mm = sem("wsel_mm")
        bias0_mm = sem("bias0_mm")
        wsel_ready = sem("wsel_ready")
        emb_mm = sem("emb_mm")
        emb_ready = sem("emb_ready")
        bi_mm = sem("bi_mm")
        bi_ready = sem("bi_ready")
        fm_ready = sem("fm_ready")
        preset = sem("preset")
        dchain = sem("dve_chain")
        achain = sem("act_chain")
        pchain = sem("pool_chain")
        stored = sem("stored")

        def reuse(eng, name, t):
            readers, rt = PREVIOUS.get((name, t), ([], 0))
            for reader in readers:
                eng.wait_ge(done[reader], rt + 1)

        block = ctx.enter_context(nc.Block())

        @block.sync
        def _(sp):
            t1 = COL["wqk1"][0]
            t3 = COL["wqk3"][0]
            sp.dma_start(idx2[:], bass.AP(a["idx2"].tensor, 0, [[0, E2], [1, B]])).then_inc(loaded["idx2"], 16)
            sp.dma_start(idx0[:], bass.AP(a["idx0"].tensor, 0, [[0, E0 + 1], [1, B]])).then_inc(loaded["small0"], 16)
            sp.dma_start(tab[:, 0:t1], a["tab"][:, 0:t1]).then_inc(loaded["tab0"], 16)
            sp.dma_start(experts0[:], a["experts0"]).then_inc(loaded["small0"], 16)
            sp.dma_start(evec0[:], a["evec0"]).then_inc(loaded["small0"], 16)
            sp.dma_start(xt[:].rearrange("p t s -> p (t s)"), a["xt"]).then_inc(loaded["xt"], 16)
            sp.dma_start(up33[:], a["up33"]).then_inc(loaded["small0"], 16)
            sp.dma_start(x_in[:], a["x"].rearrange("t p d -> p t d")).then_inc(loaded["x"], 16)
            sp.dma_start(idx1[:], bass.AP(a["idx1"].tensor, 0, [[0, P], [1, B]])).then_inc(loaded["small1"], 16)
            sp.dma_start(ada_b[:], bass.AP(a["ada_b"].tensor, 0, [[0, B], [1, 2 * D]])).then_inc(loaded["small1"], 16)
            sp.dma_start(rep[:], a["rep"]).then_inc(loaded["small1"], 16)
            sp.dma_start(rows[:], bass.AP(a["rows"].tensor, 0, [[0, P], [1, NROW]])).then_inc(loaded["rows"], 16)
            sp.dma_start(tab[:, t1:t3], a["tab"][:, t1:t3]).then_inc(loaded["tab1"], 16)
            sp.dma_start(mask_u8[:], a["mask"]).then_inc(loaded["mask"], 16)
            sp.dma_start(evec2[:], a["evec2"]).then_inc(loaded["evec2"], 16)
            for t in range(SLOTS):
                sp.dma_start(fm[:, t % SLOTS].rearrange("p h k -> p (h k)"), a["fside"][t]).then_inc(s_fs[t], 16)
            sp.dma_start(gate[:], a["gate"]).then_inc(loaded["gate"], 16)
            sp.dma_start(tab[:, t3:NCOL], a["tab"][:, t3:NCOL]).then_inc(loaded["tab3"], 16)
            sp.wait_ge(eidx_ready, 1)

            def load_experts(t):
                for b in range(NB):
                    e = sp.value_load(eidx[0:1, t * NB + b:t * NB + b + 1], min_val=0, max_val=E2 - 1)
                    sp.dma_start(wexp[:, t % WSLOTS, b, :],
                                 a["wexp"][bass.ds(e, 1), :, :].rearrange("o p n -> (o p) n")).then_inc(s_we[t], 16)

            for t in range(WSLOTS):
                load_experts(t)
            for t in range(SLOTS, NT):
                sp.wait_ge(done["sb1"], t - SLOTS + 1)
                sp.dma_start(fm[:, t % SLOTS].rearrange("p h k -> p (h k)"), a["fside"][t]).then_inc(s_fs[t], 16)
            for t in range(WSLOTS, NT):
                sp.wait_ge(done["e2"], t - WSLOTS + 1)
                load_experts(t)
            for t in range(NT):
                sp.wait_ge(done["gate"], t + 1)
                sp.dma_start(out[t], nrm[:, t, :]).then_inc(stored, 16)
            sp.wait_ge(stored, 16 * NT)

        @block.tensor
        def _(pe):
            pe.wait_ge(loaded["small0"], 64)
            pe.wait_ge(oh0_ready, 1)
            for o in range(A):
                mm = pe.matmul(bank[3 + o // 16][0:A, (o % 16) * B:(o % 16 + 1) * B],
                               experts0[:, o * A:(o + 1) * A], oh0[:, 0, :], start=True, stop=True)
            mm.then_inc(wsel_mm, 1)
            pe.matmul(bank[5][0:A, 0:B], evec0[:, 0:A], oh0[:, 0, :], start=True, stop=False)
            pe.matmul(bank[5][0:A, 0:B], evec0[:, A:2 * A], oh0[:, 1, :], start=False, stop=True).then_inc(bias0_mm, 1)

            def once_emb():
                pe.wait_ge(silu_ready, 1)
                pe.wait_ge(loaded["tab0"], 16)
                pe.matmul(bank[6][0:B, 0:2 * D], silu_t[:], col("w_ada"), start=True, stop=True).then_inc(emb_mm, 1)

            def once_bi():
                pe.wait_ge(oh2_ready, 1)
                pe.wait_ge(loaded["evec2"], 16)
                for c in range(C):
                    mm = pe.matmul(bank[7][:, c * B:(c + 1) * B], evec2[:, c * P:(c + 1) * P], oh2[:, :, 0],
                                   start=True, stop=True)
                mm.then_inc(bi_mm, 1)

            once_emb()
            once_bi()
            pe.wait_ge(wsel_ready, 1)
            pe.wait_ge(emb_ready, 1)
            pe.wait_ge(bi_ready, 1)
            pe.wait_ge(preset, 4)
            pe.wait_ge(loaded["xt"], 16)

            def transpose(dst, src):
                return pe.transpose(dst, src, ident)

            for name, engine, t in ORDER:
                if engine != "pe":
                    continue
                k = t % SLOTS
                ps = bank[BANK[name][0]]
                reuse(pe, name, t)
                layer = name[-1]
                if name == "down":
                    mm = pe.matmul(ps[0:A, 0:P], col("down_wt"), xt[:, t, :], start=True, stop=True)
                elif name == "expert":
                    pe.wait_ge(done["gelu0"], t + 1)
                    for b in range(NB):
                        mm = pe.matmul(ps[0:A, b * S:(b + 1) * S], wsel[:, :, t * NB + b],
                                       hid[:, t, b * S:(b + 1) * S], start=True, stop=True)
                elif name == "up":
                    pe.wait_ge(done["expert_bias"], t + 1)
                    mm = pe.matmul(ps[:, 0:D], hid2[:, t, :], up33[:], start=True, stop=True)
                elif name == "ada":
                    mm = pe.matmul(ps[:, 0:2 * D], rep[:, t * P:(t + 1) * P], emb[:], start=True, stop=True)
                elif name in ("tr_b", "tr_d"):
                    pe.wait_ge(done["aff_b" if name == "tr_b" else "res2"], t + 1)
                    mm = transpose(ps[:, 0:P], res[:, t, :])
                elif name in ("tr_c", "tr_f", "tr_g"):
                    pe.wait_ge(done["norm_" + layer], t + 1)
                    mm = transpose(ps[:, 0:P], nrm[:, t, :])
                elif name in ("qk1", "qk3"):
                    if t == 0:
                        pe.wait_ge(loaded["tab" + layer], 16)
                    pe.wait_ge(done["ev_b" if layer == "1" else "ev_f"], t + 1)
                    mm = pe.matmul(ps[:, 0:2 * D], xt[:, t, :], col("wqk" + layer), start=True, stop=True)
                elif name in ("v1", "v3"):
                    pe.wait_ge(done["xr" + layer], t + 1)
                    for b in range(NB):
                        mm = pe.matmul(ps[:, b * D:(b + 1) * D], xr[:, k, b, :], col("wv" + layer),
                                       start=True, stop=True)
                elif name in ("sc1", "sc3"):
                    pe.wait_ge(done["qbd" + layer], t + 1)
                    pe.wait_ge(done["kex" + layer], t + 1)
                    for g in range(HG):
                        mm = pe.matmul(ps[:, g * P:(g + 1) * P], qbd[:, k, g].rearrange("p b s -> p (b s)"),
                                       kex[:, k, g].rearrange("p h s -> p (h s)"), start=True, stop=True)
                elif name in ("pt1", "pt3"):
                    pe.wait_ge(done["exp" + layer], t + 1)
                    for g in range(HG):
                        mm = transpose(ps[:, g * P:(g + 1) * P],
                                       sc[:, k, g * H4:(g + 1) * H4, :].rearrange("p h s -> p (h s)"))
                elif name in ("ctx1", "ctx3"):
                    pe.wait_ge(done["evpt" + layer], t + 1)
                    pe.wait_ge(done["vbd" + layer], t + 1)
                    for g in range(HG):
                        for b in range(NB):
                            mm = pe.matmul(ps[b * S:(b + 1) * S, g * VW:(g + 1) * VW],
                                           pt[:, k, g, b * S:(b + 1) * S], vbd[:, k, b, g, :], start=True, stop=True,
                                           tile_position=(0, b * S))
                elif name in ("ct1", "ct3"):
                    pe.wait_ge(done["cn" + layer], t + 1)
                    mm = transpose(ps[:, 0:P], cx[:, k, :])
                elif name in ("wo1", "wo3"):
                    pe.wait_ge(done["evct" + layer], t + 1)
                    mm = pe.matmul(ps[:, 0:D], cxt[:, k, :], col("wo" + layer), start=True, stop=True)
                elif name in ("ff1", "ff3"):
                    pe.wait_ge(done["ev_c" if layer == "1" else "ev_g"], t + 1)
                    for c in range(C):
                        mm = pe.matmul(ps[:, c * P:(c + 1) * P], col("w1" + layer, c * P, P), xt[:, t, :],
                                       start=True, stop=True)
                elif name in ("fo1", "fo3"):
                    pe.wait_ge(done["act" + layer], t + 1)
                    for c in range(C):
                        mm = pe.matmul(ps[:, 0:D], hg[:, k, c, :], col("w2" + layer, c * D, D),
                                       start=(c == 0), stop=(c == C - 1))
                elif name == "sel":
                    mm = pe.matmul(ps[:, 0:3 * D], oh2[:, t * NB:(t + 1) * NB, :].rearrange("e b s -> e (b s)"),
                                   evec2[:, FF:FF + 3 * D], start=True, stop=True)
                elif name == "e1":
                    pe.wait_ge(done["ev_d"], t + 1)
                    pe.wait_ge(s_we[t], 16 * NB)
                    for b in range(NB):
                        mm = pe.matmul(ps[b * S:(b + 1) * S, :], xt[:, t, b * S:(b + 1) * S],
                                       wexp[:, t % WSLOTS, b, 0:FF], start=True, stop=True, tile_position=(0, b * S))
                elif name == "et":
                    pe.wait_ge(done["eve1"], t + 1)
                    for c in range(C):
                        mm = transpose(ps[:, c * P:(c + 1) * P], pt[:, k, c, :])
                elif name == "e2":
                    pe.wait_ge(done["gelu2"], t + 1)
                    for c in range(C):
                        for b in range(NB):
                            mm = pe.matmul(ps[b * S:(b + 1) * S, 0:D], hg[:, k, c, b * S:(b + 1) * S],
                                           wexp[:, t % WSLOTS, b, FF + c * D:FF + (c + 1) * D],
                                           start=(c == 0), stop=(c == C - 1), tile_position=(0, b * S))
                mm.then_inc(done[name], 1)

        @block.scalar
        def _(act):
            chain = [0]

            def link(ins):
                chain[0] += 1
                ins.then_inc(achain, 1)
                act.wait_ge(achain, chain[0])

            act.wait_ge(angle_ready, 1)
            link(act.activation(silu_t[:], ang[:, 0, :], ACT.Sin))
            act.activation(silu_t[:], silu_t[:], ACT.Silu).then_inc(silu_ready, 1)
            act.wait_ge(preset, 4)
            act.wait_ge(loaded["tab0"], 16)
            table = ["none"]
            for name, engine, t in ORDER:
                if engine != "act":
                    continue
                k = t % SLOTS
                layer = name[-1]
                reuse(act, name, t)
                if name == "gelu0":
                    act.wait_ge(done["down"], t + 1)
                    table[0] = "gelu"
                    ins = act.activation(hid[:, t, :], bank[0][0:A, 0:P], ACT.Gelu, bias=cvec(C_DOWN_B, A))
                elif name.startswith("rstd"):
                    act.wait_ge(done["stat_" + layer], t + 1)
                    if table[0] != "ln":
                        act.preload_act_table_set("natural_log_exp_and_others")
                        table[0] = "ln"
                    link(act.activation(lnv[:, t:t + 1], mv[:, t, 1:2], ACT.Ln,
                                        bias=eps[:, 1:2] if layer == "e" else eps[:, 0:1]))
                    ins = act.activation(rstd[:, t:t + 1], lnv[:, t:t + 1], ACT.Exp, scale=-0.5)
                elif name in ("ev_b", "ev_d"):
                    act.wait_ge(done["tr_" + layer], t + 1)
                    ins = act.activation(xt[:, t, :], bank[0][:, 0:P], ACT.Copy)
                elif name in ("ev_c", "ev_f", "ev_g"):
                    act.wait_ge(done["tr_" + layer], t + 1)
                    s_, b_ = {"c": (C_G2, C_BETA2), "f": (C_G31, C_B31), "g": (C_G32, C_B32)}[layer]
                    ins = act.activation(xt[:, t, :], bank[0][:, 0:P], ACT.Identity, bias=cvec(b_), scale=cvec(s_))
                elif name in ("xr1", "xr3"):
                    act.wait_ge(done["ev_b" if layer == "1" else "ev_f"], t + 1)
                    ins = act.activation(
                        xr[:, k].rearrange("p b (r s) -> p b r s", r=H4),
                        xt[:, t, :].rearrange("p (b s) -> p b s", b=NB)[:, :, None, :].broadcast_to([P, NB, H4, S]),
                        ACT.Copy)
                elif name in ("exp1", "exp3"):
                    act.wait_ge(done["sub" + layer], t + 1)
                    if table[0] != "ln":
                        act.preload_act_table_set("natural_log_exp_and_others")
                        table[0] = "ln"
                    ins = act.activation(sc[:, k], sc[:, k], ACT.Exp)
                elif name in ("evpt1", "evpt3"):
                    act.wait_ge(done["pt" + layer], t + 1)
                    ins = act.activation(pt[:, k].rearrange("p c q -> p (c q)"), bank[5][:], ACT.Copy)
                elif name in ("evct1", "evct3"):
                    act.wait_ge(done["ct" + layer], t + 1)
                    ins = act.activation(cxt[:, k, :], bank[0][:, 0:P], ACT.Identity,
                                         bias=cvec(C_BV1 if layer == "1" else C_BV3))
                elif name in ("act1", "act3"):
                    act.wait_ge(done["ff" + layer], t + 1)
                    table[0] = "gelu"
                    for c in range(C):
                        ins = act.activation(hg[:, k, c, :], bank[7][:, c * P:(c + 1) * P],
                                             ACT.Gelu_apprx_sigmoid if layer == "1" else ACT.Gelu,
                                             bias=cvec((C_B1_1 if layer == "1" else C_B1_3) + c))
                elif name == "evsel":
                    act.wait_ge(done["sel"], t + 1)
                    ins = act.activation(selv[:, k, :], bank[1][:, 0:3 * D], ACT.Copy)
                elif name == "eve1":
                    act.wait_ge(done["e1"], t + 1)
                    ins = act.activation(pt[:, k].rearrange("p c q -> p (c q)"), bank[3][:], ACT.Copy)
                elif name == "gelu2":
                    act.wait_ge(done["eb"], t + 1)
                    table[0] = "gelu"
                    ins = act.activation(hg[:, k], hg[:, k], ACT.Gelu)
                ins.then_inc(done[name], 1)

        @block.vector
        def _(dve):
            chain = [0]

            def link(ins):
                chain[0] += 1
                ins.then_inc(dchain, 1)
                dve.wait_ge(dchain, chain[0])

            dve.memset(hid2[A:A + 1, :, :], 1.0).then_inc(preset, 1)
            dve.memset(eps[:, 0:1], EPS).then_inc(preset, 1)
            dve.memset(eps[:, 1:2], EPS2).then_inc(preset, 1)
            dve.wait_ge(loaded["idx2"], 16)
            link(dve.tensor_copy(f2[:, 0, :], idx2[:]))
            link(dve.tensor_scalar(f2[:, 1, :], f2[:, 0, :], 0.0, float(E2), ALU.is_lt, ALU.mult))
            link(dve.tensor_tensor(f2[:, 2, :], f2[:, 0, :], f2[:, 1, :], ALU.add))
            link(dve.tensor_scalar(f2[:, 3, :], f2[:, 2, :], 0.0, float(E2 - 1), ALU.max, ALU.min))
            dve.tensor_copy(eidx[:], f2[0:1, 3, :]).then_inc(eidx_ready, 1)
            dve.wait_ge(loaded["small0"], 64)
            dve.wait_ge(loaded["tab0"], 16)
            link(dve.tensor_copy(f0[:, 0, :], idx0[:]))
            link(dve.tensor_scalar(f0[:, 1, :], f0[:, 0, :], 0.0, float(E0 - 1), ALU.max, ALU.min))
            link(dve.tensor_tensor(f0[:, 2, :], f0[:, 0, :], f0[:, 1, :], ALU.not_equal))
            link(dve.tensor_scalar(f0[:, 3, :], f0[:, 2, :], float(E0 + 1), None, ALU.mult))
            link(dve.tensor_tensor(f0[:, 2, :], f0[:, 1, :], f0[:, 3, :], ALU.add))
            link(dve.tensor_scalar(f0[:, 3, :], f0[:, 2, :], float(E0), None, ALU.min))
            dve.tensor_scalar(oh0[:, 0, :], f0[:, 3, :], cvec(C_IOTA, E0 + 1), None, ALU.is_equal)
            dve.tensor_scalar(oh0[:, 1, :], f0[:, 1, :], cvec(C_IOTA, E0 + 1), None, ALU.is_equal).then_inc(oh0_ready, 1)
            dve.wait_ge(loaded["small1"], 48)
            link(dve.tensor_copy(ang[:, 0, :], idx1[:]))
            link(dve.tensor_scalar(ang[:, 1, :], ang[:, 0, :], 40.0, cvec(C_FREQ), ALU.mult, ALU.mult))
            link(dve.tensor_scalar(ang[:, 2, :], ang[:, 1, :], cvec(C_PHASE), 1.0 / TWO_PI, ALU.add, ALU.mult))
            link(dve.tensor_scalar(ang[:, 3, :], ang[:, 2, :], ROUND, ROUND, ALU.add, ALU.subtract))
            link(dve.scalar_tensor_tensor(ang[:, 0, :], ang[:, 3, :], -PI_A, ang[:, 1, :], ALU.mult, ALU.add))
            link(dve.scalar_tensor_tensor(ang[:, 1, :], ang[:, 3, :], -PI_B, ang[:, 0, :], ALU.mult, ALU.add))
            link(dve.scalar_tensor_tensor(ang[:, 2, :], ang[:, 3, :], -PI_C, ang[:, 1, :], ALU.mult, ALU.add))
            link(dve.tensor_scalar(ang[:, 1, :], ang[:, 2, :], cvec(C_PHASE), 3.1415925, ALU.add, ALU.min))
            dve.tensor_scalar(ang[:, 0, :], ang[:, 1, :], -3.1415925, None, ALU.max).then_inc(angle_ready, 1)
            link(dve.tensor_scalar(oh2[:, :, 0], f2[:, 3, :], cvec(C_IOTA, E2), None, ALU.is_equal))
            dve.tensor_copy(oh2[:, :, 1:S], oh2[:, :, 0:1].broadcast_to([E2, B, S - 1])).then_inc(oh2_ready, 1)
            dve.wait_ge(wsel_mm, 1)
            for n in range(2):
                dve.tensor_copy(wsel[:, 16 * n:16 * n + 16, :].rearrange("a o b -> a (o b)"), bank[3 + n][0:A, :])
            dve.wait_ge(bias0_mm, 1)
            dve.tensor_copy(bias0[:], bank[5][0:A, 0:B]).then_inc(wsel_ready, 1)
            dve.wait_ge(emb_mm, 1)
            dve.tensor_tensor(emb[:], bank[6][0:B, 0:2 * D], ada_b[:], ALU.add).then_inc(dchain, 1)
            chain[0] += 1
            dve.wait_ge(dchain, chain[0])
            dve.tensor_scalar(emb[:, 0:D], emb[:, 0:D], 1.0, None, ALU.add).then_inc(emb_ready, 1)
            dve.wait_ge(bi_mm, 1)
            dve.tensor_copy(bi_sel[:].rearrange("p c b -> p (c b)"), bank[7][:, 0:C * B]).then_inc(bi_ready, 1)
            dve.wait_ge(wsel_ready, 1)
            dve.wait_ge(preset, 4)
            dve.wait_ge(loaded["x"], 16)
            dve.wait_ge(loaded["rows"], 16)
            dve.wait_ge(loaded["gate"], 16)

            prev_norm = {"a": "res0", "b": "aff_a", "c": "res1", "e": "res3", "f": "aff_e", "g": "res4"}
            for name, engine, t in ORDER:
                if engine != "dve":
                    continue
                k = t % SLOTS
                layer = name[-1]
                reuse(dve, name, t)
                if name == "expert_bias":
                    dve.wait_ge(done["expert"], t + 1)
                    ins = dve.tensor_tensor(
                        hid2[0:A, t, :].rearrange("o (b s) -> o b s", b=NB),
                        bank[1][0:A, 0:P].rearrange("o (b s) -> o b s", b=NB),
                        bias0[:, t * NB:(t + 1) * NB, None].broadcast_to([A, NB, S]), ALU.add)
                elif name == "res0":
                    dve.wait_ge(done["up"], t + 1)
                    ins = dve.tensor_tensor(res[:, t, :], bank[2][:, 0:D], x_in[:, t, :], ALU.add)
                elif name.startswith("stat"):
                    dve.wait_ge(done[prev_norm[layer]], t + 1)
                    link(dve.bn_stats(bn[:, t, :], res[:, t, :]))
                    ins = dve.bn_aggr(mv[:, t, :], bn[:, t, :])
                elif name.startswith("norm"):
                    dve.wait_ge(done["rstd_" + layer], t + 1)
                    ins = dve.tensor_scalar(nrm[:, t, :], res[:, t, :], mv[:, t, 0:1], rstd[:, t:t + 1],
                                            ALU.subtract, ALU.mult)
                elif name == "aff_b":
                    dve.wait_ge(done["norm_b"], t + 1)
                    dve.wait_ge(done["ada"], t + 1)
                    link(dve.tensor_tensor(res[:, t, :], nrm[:, t, :], bank[1][:, 0:D], ALU.mult))
                    ins = dve.tensor_tensor(res[:, t, :], res[:, t, :], bank[1][:, D:2 * D], ALU.add)
                elif name in ("qkb1", "qkb3"):
                    dve.wait_ge(done["qk" + layer], t + 1)
                    ins = dve.tensor_tensor(qk[:, k, :], bank[1][:, 0:2 * D], row("bqk" + layer, 2 * D), ALU.add)
                elif name in ("qkt1", "qkt3"):
                    dve.wait_ge(done["qkb" + layer], t + 1)
                    ins = dve.transpose(qkt[:, k].rearrange("p j g s -> p (j g s)"), qk[:, k, :])
                elif name in ("kex1", "kex3"):
                    dve.wait_ge(done["qkt" + layer], t + 1)
                    ins = dve.tensor_tensor(kex[:, k], qkt[:, k, 1, :, None, :].broadcast_to([P, HG, H4, S]),
                                            col("head_mask")[:, None, :, None].broadcast_to([P, HG, H4, S]), ALU.mult)
                elif name in ("vbd1", "vbd3"):
                    dve.wait_ge(done["v" + layer], t + 1)
                    n = NB * HG
                    ins = dve.tensor_tensor(
                        vbd[:, k].rearrange("p b g w -> p (b g) w")[:, :, 0:H4 * DH].rearrange(
                            "p n (h d) -> p n h d", h=H4),
                        bank[3][:].rearrange("p (n h d) -> p n h d", n=n, h=H4),
                        col("seq_mask")[:, None, :, None].broadcast_to([P, n, H4, DH]), ALU.mult)
                elif name in ("sb1", "sb3"):
                    dve.wait_ge(done["sc" + layer], t + 1)
                    if layer == "1":
                        dve.wait_ge(fm_ready, t + 1)
                        bias = fm[:, t % SLOTS]
                    else:
                        bias = col("causal")[:, None, :].broadcast_to([P, H, S])
                    ins = dve.tensor_tensor(sc[:, k], bank[4][:].rearrange("p (h s) -> p h s", h=H), bias, ALU.add)
                elif name in ("mx1", "mx3"):
                    dve.wait_ge(done["sb" + layer], t + 1)
                    ins = dve.tensor_reduce(mx[:, t, :], sc[:, k], AX.X, ALU.max)
                elif name in ("cn1", "cn3"):
                    dve.wait_ge(done["ctx" + layer], t + 1)
                    p4 = bank[6][:, 0:HG * VW].rearrange("p (g w) -> p g w", g=HG)
                    link(dve.reciprocal(rsum[:, t, :].rearrange("p (g h) -> p g h", g=HG), p4[:, :, H4 * DH:VW]))
                    ins = dve.tensor_tensor(
                        cx[:, k, :].rearrange("p (g h d) -> p g h d", g=HG, h=H4),
                        p4[:, :, 0:H4 * DH].rearrange("p g (h d) -> p g h d", h=H4),
                        rsum[:, t, :].rearrange("p (g h) -> p g h", g=HG)[:, :, :, None].broadcast_to(
                            [P, HG, H4, DH]), ALU.mult)
                elif name in ("res1", "res4"):
                    l_ = "1" if name == "res1" else "3"
                    dve.wait_ge(done["wo" + l_], t + 1)
                    dve.wait_ge(done["xbo" + l_], t + 1)
                    ins = dve.tensor_tensor(res[:, t, :] if l_ == "1" else res[:, t, :], bank[2][:, 0:D],
                                            resb[:, t, :], ALU.add)
                elif name == "res2":
                    dve.wait_ge(done["fo1"], t + 1)
                    dve.wait_ge(done["xb21"], t + 1)
                    ins = dve.tensor_tensor(res[:, t, :], bank[6][:, 0:D], resb[:, t, :], ALU.add)
                elif name == "eb":
                    dve.wait_ge(done["et"], t + 1)
                    ins = dve.tensor_tensor(
                        hg[:, k].rearrange("p c (b s) -> p c b s", b=NB),
                        bank[5][:].rearrange("p (c b s) -> p c b s", c=C, b=NB),
                        bi_sel[:, :, t * NB:(t + 1) * NB, None].broadcast_to([P, C, NB, S]), ALU.add)
                elif name == "res3":
                    dve.wait_ge(done["e2"], t + 1)
                    dve.wait_ge(done["xbo2"], t + 1)
                    ins = dve.tensor_tensor(res[:, t, :], bank[6][:, 0:D], resb[:, t, :], ALU.add)
                elif name == "res5":
                    dve.wait_ge(done["fo3"], t + 1)
                    dve.wait_ge(done["xb23"], t + 1)
                    ins = dve.tensor_tensor(resb[:, t, :], bank[6][:, 0:D], resb[:, t, :], ALU.add)
                elif name == "gate":
                    dve.wait_ge(done["res5"], t + 1)
                    ins = dve.scalar_tensor_tensor(nrm[:, t, :], resb[:, t, :], gate[:, t:t + 1], x_in[:, t, :],
                                                   ALU.mult, ALU.add)
                ins.then_inc(done[name], 1)

        @block.gpsimd
        def _(pool):
            chain = [0]

            def link(ins):
                chain[0] += 1
                ins.then_inc(pchain, 1)
                pool.wait_ge(pchain, chain[0])

            pool.wait_ge(loaded["tab0"], 16)
            pool.tensor_copy(
                vbd[:].rearrange("p k b g w -> p (k b g) w")[:, :, H4 * DH:VW],
                col("seq_mask")[:, None, :].broadcast_to([P, SLOTS * NB * HG, H4])).then_inc(preset, 1)
            pool.wait_ge(loaded["mask"], 16)
            link(pool.tensor_scalar(mask_add[:].rearrange("p t k -> p (t k)"), mask_u8[:], NEG, None, ALU.mult))
            pool.wait_ge(loaded["rows"], 16)
            fm_done = 0
            for name, engine, t in ORDER:
                if engine != "pool":
                    continue
                k = t % SLOTS
                layer = name[-1]
                reuse(pool, name, t)
                if name == "aff_a":
                    pool.wait_ge(done["norm_a"], t + 1)
                    link(pool.tensor_tensor(res[:, t, :], nrm[:, t, :], row("g0"), ALU.mult))
                    ins = pool.tensor_tensor(res[:, t, :], res[:, t, :], row("be0"), ALU.add)
                elif name == "aff_e":
                    pool.wait_ge(done["norm_e"], t + 1)
                    link(pool.tensor_tensor(res[:, t, :], nrm[:, t, :], selv[:, k, D:2 * D], ALU.mult))
                    link(pool.tensor_tensor(res[:, t, :], res[:, t, :], selv[:, k, 2 * D:3 * D], ALU.add))
                    ins = pool.tensor_copy(x_in[:, t, :], res[:, t, :])
                elif name in ("xbo1", "xbo3"):
                    pool.wait_ge(done["aff_b" if layer == "1" else "aff_e"], t + 1)
                    ins = pool.tensor_tensor(resb[:, t, :], res[:, t, :], row("bo" + layer), ALU.add)
                    if layer == "1":
                        ins.then_inc(done[name], 1)
                        pool.wait_ge(s_fs[t], 16)
                        pool.tensor_tensor(fm[:, t % SLOTS], fm[:, t % SLOTS], mask_add[:, t, None, :].broadcast_to([P, H, S]),
                                           ALU.add).then_inc(fm_ready, 1)
                        continue
                elif name in ("qbd1", "qbd3"):
                    pool.wait_ge(done["qkt" + layer], t + 1)
                    at = COL["cvec"][0] + 20
                    ins = pool.tensor_tensor(qbd[:, k], qkt[:, k, 0, :, None, :].broadcast_to([P, HG, NB, S]),
                                             tab[:, None, at:at + NB, None].broadcast_to([P, HG, NB, S]), ALU.mult)
                elif name in ("sub1", "sub3"):
                    pool.wait_ge(done["mx" + layer], t + 1)
                    ins = pool.tensor_tensor(sc[:, k], sc[:, k], mx[:, t, :, None].broadcast_to([P, H, S]),
                                             ALU.subtract)
                elif name == "xb21":
                    pool.wait_ge(done["res1"], t + 1)
                    ins = pool.tensor_tensor(resb[:, t, :], res[:, t, :], row("b21"), ALU.add)
                elif name == "xbo2":
                    pool.wait_ge(done["res2"], t + 1)
                    pool.wait_ge(done["evsel"], t + 1)
                    ins = pool.tensor_tensor(resb[:, t, :], res[:, t, :], selv[:, k, 0:D], ALU.add)
                elif name == "xb23":
                    pool.wait_ge(done["res4"], t + 1)
                    link(pool.tensor_tensor(resb[:, t, :], res[:, t, :], row("b23"), ALU.add))
                    ins = pool.tensor_tensor(resb[:, t, :], resb[:, t, :], x_in[:, t, :], ALU.subtract)
                ins.then_inc(done[name], 1)


def kernel(**inputs):
    import numpy as np
    import concourse.bacc as _bacc
    from concourse import mybir as _mybir
    from concourse.bass_utils import run_bass_kernel_spmd as _run

    v = {n: np.asarray(a) for n, a in inputs.items()}
    f = np.float32

    def cols(a):
        return np.ascontiguousarray(a.reshape(-1, P).T)

    def chunks(w):
        return w.reshape(C, P, -1).transpose(1, 0, 2).reshape(P, -1)

    p = np.arange(P)
    cvec = np.zeros((P, 32), f)
    cvec[0:A, C_DOWN_B] = v["L0_cond_down_b"]
    half = D // 2
    freqs = np.exp(np.arange(half, dtype=f) * f(-math.log(10000.0) / (half - 1))).astype(f)
    cvec[:, C_FREQ] = np.concatenate([freqs, freqs])
    cvec[half:, C_PHASE] = math.pi / 2
    cvec[:, C_IOTA] = p
    for i, n in ((C_BV1, "L1_cond_bv"), (C_G2, "L1_cond_g2"), (C_BETA2, "L1_cond_beta2"), (C_BV3, "L3_cond_bv"),
                 (C_G31, "L3_cond_gamma1"), (C_B31, "L3_cond_beta1"), (C_G32, "L3_cond_gamma2"),
                 (C_B32, "L3_cond_beta2")):
        cvec[:, i] = v[n]
    cvec[:, C_B1_1:C_B1_1 + C] = cols(v["L1_cond_b1"])
    cvec[:, C_B1_3:C_B1_3 + C] = cols(v["L3_cond_b1"])
    seq_mask = (p[:, None] // S == np.arange(NB)[None, :]).astype(f)
    cvec[:, 20:20 + NB] = seq_mask * f(1.0 / math.sqrt(DH))
    parts = {
        "ident": np.eye(P, dtype=f), "down_wt": v["L0_cond_down_W"].T, "seq_mask": seq_mask,
        "head_mask": ((p[:, None] % S) // DH == np.arange(H4)[None, :]).astype(f), "cvec": cvec,
        "w_ada": v["L1_cond_W_ada"],
        "causal": np.where(np.arange(S)[None, :] <= (p % S)[:, None], 0.0, NEG).astype(f),
    }
    for l in "13":
        w = {n: v[f"L{l}_cond_{n}"] for n in ("Wq", "Wk", "Wv", "Wo", "W1", "W2")}
        parts.update({"wqk" + l: np.concatenate([w["Wq"], w["Wk"]], 1), "wv" + l: w["Wv"], "wo" + l: w["Wo"],
                      "w1" + l: w["W1"], "w2" + l: chunks(w["W2"])})
    tab = np.concatenate([parts[n] for n, _ in COLS], 1)
    rows = np.concatenate([v[n] for n in (
        "L0_cond_ln_gamma", "L0_cond_ln_beta", "L1_cond_bq", "L1_cond_bk", "L1_cond_bo", "L1_cond_b2",
        "L3_cond_bq", "L3_cond_bk", "L3_cond_bo", "L3_cond_b2")])
    experts0 = np.concatenate([v["L0_cond_expert_W"].reshape(E0, A * A), np.eye(A, dtype=f).reshape(1, A * A)])
    evec0 = np.concatenate([np.concatenate([v["L0_cond_expert_b"], v["L0_cond_domain_emb"]], 1),
                            np.zeros((1, 2 * A), f)])
    wi = v["L2_cond_Wi"]
    wo = v["L2_cond_Wo"].reshape(E2, C, P, D).transpose(0, 2, 1, 3).reshape(E2, P, C * D)
    rep = (np.arange(B)[:, None] == (np.arange(NT * P) // S)[None, :]).astype(f)
    laid = {
        "x": v["x"].reshape(NT, P, D),
        "xt": v["x"].reshape(NT * P, D).T,
        "tab": tab, "rows": rows, "experts0": experts0, "evec0": evec0,
        "up33": np.concatenate([v["L0_cond_up_W"].T, v["L0_cond_up_b"][None]]),
        "ada_b": v["L1_cond_b_ada"], "rep": rep,
        "evec2": np.concatenate([v["L2_cond_" + n] for n in ("bi", "bo", "gamma", "beta")], 1),
        "wexp": np.concatenate([wi, wo], 2),
        "fside": v["fside_Bx16xSxS_0"].reshape(NT, NB, H, S, S).transpose(0, 1, 3, 2, 4).reshape(NT, P, H * S),
        "mask": v["mask_Bx1xSxS_bk0"].reshape(NT, P, S).transpose(1, 0, 2).reshape(P, NT * S),
        "idx0": v["itok_B_0_15"], "idx1": v["itok_B_34_63"], "idx2": v["itok_B_0_7"],
        "gate": np.repeat(v["condB_gatescore"], S).reshape(NT, P).T,
    }
    nc = _bacc.Bacc("TRN2", target_bir_lowering=False, num_devices=1)
    arrays, aps = {}, {}
    for name, x in laid.items():
        x = np.ascontiguousarray(x)
        arrays[f"in_{name}"] = x
        aps[name] = nc.dram_tensor(f"in_{name}", x.shape, _mybir.dt.from_np(x.dtype), kind="ExternalInput").ap()
    out = nc.dram_tensor("out_0", (NT, P, D), _mybir.dt.float32, kind="ExternalOutput").ap()
    build(nc, aps, out)
    r = _run(nc, [arrays], core_ids=[0])
    return r.results[0]["out_0"].reshape(B, S, D)
```

```python
import math
from contextlib import ExitStack

import concourse.bass as bass
from concourse import mybir

F32 = mybir.dt.float32
I32 = mybir.dt.int32
U8 = mybir.dt.uint8
ALU = mybir.AluOpType
ACT = mybir.ActivationFunctionType
AX = mybir.AxisListType

P = 128
B, S, D = 32, 32, 128
NB = P // S
NT = B // NB
H, DH = 16, 8
HG = 4
H4 = H // HG
A = 32
E0, E2 = 16, 8
FF = 512
C = FF // P
VW = H4 * DH + H4
SLOTS = 4
EPS = 1e-5
EPS2 = 1e-12
NEG = -1e30
TWO_PI = 2 * math.pi
PI_A = 6.28125
PI_B = 0.00193500518798828125
PI_C = TWO_PI - PI_A - PI_B
ROUND = 1.5 * 2.0**23

COLS = [
    ("ident", P), ("down_wt", A), ("seq_mask", NB), ("head_mask", H4), ("cvec", 32),
    ("w_ada", 2 * D), ("causal", S),
    ("wqkv1", 3 * D), ("wo1", D), ("w11", FF), ("w21", FF),
    ("wqkv3", 3 * D), ("wo3", D), ("w13", FF), ("w23", FF),
]
COL = {}
_at = 0
for _n, _w in COLS:
    COL[_n] = (_at, _w)
    _at += _w
NCOL = _at
(C_DOWN_B, C_FREQ, C_PHASE, C_IOTA, C_BV1, C_G2, C_BETA2, C_BV3, C_G31, C_B31, C_G32, C_B32) = range(12)
C_B1_1, C_B1_3 = 12, 16
ROWS = ["g0", "be0", "bqkv1", "bk1", "bv1", "bo1", "b21", "bqkv3", "bk3", "bv3", "bo3", "b23"]
ROW = {n: i * D for i, n in enumerate(ROWS)}
NROW = len(ROWS) * D

STEPS = """
ada    sp   100/600 -    ;
fs     sp   100/1000 -    ;
wl0    sp   500/2100 -    ; wl2@-1
wl1    sp   500/2100 -    ; wl3@-1
wl2    sp   500/2100 -    ; wl0
wl3    sp   500/2100 -    ; wl1
down   pe   300  -    ;
gelu0  act  300  gelu ; down
expert pe   424  -    ; gelu0
ebias  dve  202  -    ; expert
up     pe   300  -    ; ebias
res0   dve  202  -    ; up
stat_a dve  277  -    ; res0
rstd_a act  440  ln   ; stat_a
norm_a dve  256  -    ; rstd_a
aff_a  pool 975  -    ; norm_a
stat_b dve  277  -    ; aff_a
rstd_b act  440  ln   ; stat_b
norm_b dve  256  -    ; rstd_b
aff_b  dve  404  -    ; norm_b ada
tr_b   pe   134  -    ; aff_b
ev_b   act  158  -    ; tr_b
xbo1   pool 417  -    ; aff_b
mask1  pool 1100 -    ; fs
qkv1   pe   750  -    ; ev_b
qkvb1  dve  470  -    ; qkv1
vw1    sp   100/300  -    ; qkvb1
vr1    sp   400/1200 -    ; vw1
qkt1   dve  335  -    ; qkvb1
qbd1   pool 1001 -    ; qkt1
kex1   dve  602  -    ; qkt1
sc1    pe   900  -    ; qbd1 kex1
sb1    dve  602  -    ; sc1 mask1
mx1    dve  602  -    ; sb1
sub1   pool 1001 -    ; mx1
exp1   act  620  ln   ; sub1
pt1    pe   481  -    ; exp1
evpt1  act  478  -    ; pt1
vbd1   dve  602  -    ; vr1
ctx1   pe   560  -    ; evpt1 vbd1
cn1    dve  367  -    ; ctx1
ct1    pe   134  -    ; cn1
evct1  act  251  -    ; ct1
wo1    pe   268  -    ; evct1
res1   dve  202  -    ; wo1 xbo1
stat_c dve  277  -    ; res1
xb21   pool 417  -    ; res1
rstd_c act  440  ln   ; stat_c
norm_c dve  256  -    ; rstd_c
tr_c   pe   134  -    ; norm_c
ev_c   act  344  -    ; tr_c
ff1    pe   1000 -    ; ev_c
act1   act  1300 gas  ; ff1
fo1    pe   1050 -    ; act1
res2   dve  202  -    ; fo1 xb21
tr_d   pe   134  -    ; res2
ev_d   act  158  -    ; tr_d
xbo2   pool 417  -    ; res2 wl2 wl3
e1     pe   1200 -    ; ev_d wl2 wl3
eve1   act  478  -    ; e1
et     pe   481  -    ; eve1
eb     dve  602  -    ; et
gelu2  act  620  gelu ; eb
e2     pe   1144 -    ; gelu2
res3   dve  202  -    ; e2 xbo2
stat_e dve  277  -    ; res3
rstd_e act  440  ln   ; stat_e
norm_e dve  256  -    ; rstd_e
aff_e  pool 1381 -    ; norm_e
stat_f dve  277  -    ; aff_e
rstd_f act  440  ln   ; stat_f
norm_f dve  256  -    ; rstd_f
tr_f   pe   134  -    ; norm_f
ev_f   act  344  -    ; tr_f
xbo3   pool 417  -    ; aff_e
qkv3   pe   750  -    ; ev_f
qkvb3  dve  470  -    ; qkv3
vw3    sp   100/300  -    ; qkvb3
vr3    sp   400/1200 -    ; vw3
qkt3   dve  335  -    ; qkvb3
qbd3   pool 1001 -    ; qkt3
kex3   dve  602  -    ; qkt3
sc3    pe   900  -    ; qbd3 kex3
sb3    dve  602  -    ; sc3
mx3    dve  602  -    ; sb3
sub3   pool 1001 -    ; mx3
exp3   act  620  ln   ; sub3
pt3    pe   481  -    ; exp3
evpt3  act  478  -    ; pt3
vbd3   dve  602  -    ; vr3
ctx3   pe   560  -    ; evpt3 vbd3
cn3    dve  367  -    ; ctx3
ct3    pe   134  -    ; cn3
evct3  act  251  -    ; ct3
wo3    pe   268  -    ; evct3
res4   dve  202  -    ; wo3 xbo3
stat_g dve  277  -    ; res4
xb23   pool 834  -    ; res4
rstd_g act  440  ln   ; stat_g
norm_g dve  256  -    ; rstd_g
tr_g   pe   134  -    ; norm_g
ev_g   act  344  -    ; tr_g
ff3    pe   1000 -    ; ev_g
act3   act  1300 gelu ; ff3
fo3    pe   1050 -    ; act3
res5   dve  202  -    ; fo3 xb23
gate   dve  263  -    ; res5
store  sp   100/300  -    ; gate
"""
STEP = {}
for _line in STEPS.strip().splitlines():
    _head, _deps = _line.split(";")
    _name, _engine, _ns, _table = _head.split()
    _ns = [int(x) for x in _ns.split("/")]
    STEP[_name] = (_engine, _ns[0], _ns[-1] if len(_ns) > 1 else 0, _table, _deps.split())

DRAIN = {"down": "gelu0", "expert": "ebias", "up": "res0", "tr_b": "ev_b", "qkv1": "qkvb1", "sc1": "sb1",
         "pt1": "evpt1", "ctx1": "cn1", "ct1": "evct1", "wo1": "res1", "tr_c": "ev_c", "ff1": "act1",
         "fo1": "res2", "tr_d": "ev_d", "e1": "eve1", "et": "eb", "e2": "res3", "tr_f": "ev_f",
         "qkv3": "qkvb3", "sc3": "sb3", "pt3": "evpt3", "ctx3": "cn3", "ct3": "evct3", "wo3": "res4",
         "tr_g": "ev_g", "ff3": "act3", "fo3": "res5"}
SLOT_USES = {
    "adav": [("ada", ["aff_b"])],
    "fm": [("fs", ["sb1"])],
    "wexp02": [("wl0", ["e2", "aff_e"])],
    "wexp13": [("wl1", ["e2", "aff_e"])],
    "qkv": [("qkvb1", ["qkt1", "vw1"]), ("qkvb3", ["qkt3", "vw3"])],
    "vdram": [("vw1", ["vr1"]), ("vw3", ["vr3"])],
    "qkt": [("qkt1", ["qbd1", "kex1"]), ("qkt3", ["qbd3", "kex3"])],
    "qbd": [("qbd1", ["sc1"]), ("qbd3", ["sc3"])],
    "kex": [("kex1", ["sc1"]), ("kex3", ["sc3"])],
    "vrep": [("vr1", ["vbd1"]), ("vr3", ["vbd3"])],
    "vbd": [("vbd1", ["ctx1"]), ("vbd3", ["ctx3"])],
    "sc": [("sb1", ["pt1"]), ("sb3", ["pt3"])],
    "pt": [("evpt1", ["ctx1"]), ("eve1", ["et"]), ("evpt3", ["ctx3"])],
    "cx": [("cn1", ["ct1"]), ("cn3", ["ct3"])],
    "cxt": [("evct1", ["wo1"]), ("evct3", ["wo3"])],
    "hg": [("act1", ["fo1"]), ("eb", ["e2"]), ("act3", ["fo3"])],
}
TRANSFERS = {"ada": 1, "fs": 1,  "vw1": 1, "vr1": H4, "vw3": 1, "vr3": H4}
BANKS = 8
SIGNAL = 60
DMA_NS = 2000
TABLE_NS = 1300
TABLE_BIAS = 15000
TILE_NS = 2000
START_NS = 11000


def plan():
    succ = {n: [] for n in STEP}
    for n, (_, _, _, _, deps) in STEP.items():
        for d in deps:
            if "@" not in d:
                succ[d].append(n)
    tail = {}
    for n in reversed(list(STEP)):
        _, ns, land, _, _ = STEP[n]
        tail[n] = ns + land + SIGNAL + max([tail[m] for m in succ[n]], default=0)
    starts = {}
    for buf, uses in SLOT_USES.items():
        for writer, readers in uses:
            starts.setdefault(writer, []).append((buf, readers))
    rank = {(n, t): tail[n] - TILE_NS * t for n in STEP for t in range(NT)}
    end = {}
    owner = {}
    bank_of, previous, started, order = {}, {}, {}, []
    left = {e: [(n, t) for n in STEP for t in range(NT) if STEP[n][0] == e] for e in
            ("pe", "dve", "act", "pool", "sp")}
    free = {e: START_NS for e in left}
    free["sp"] = 0
    table = None
    dma_free = 0

    def freed(what):
        if what not in owner:
            return 0
        readers, t = owner[what]
        times = [end.get((r, t)) for r in readers]
        return None if None in times else max(times)

    while any(left.values()):
        choice = None
        for e, steps in left.items():
            able, seen = [], set()
            for n, t in steps:
                if n in seen:
                    continue
                seen.add(n)
                _, ns, land, tab, deps = STEP[n]
                inputs = [end.get((d, t)) for d in deps if "@" not in d]
                inputs += [end.get((d[:-3], t - 1)) for d in deps if "@" in d and t > 0]
                freed_at = [freed((buf, t % SLOTS)) for buf, _ in starts.get(n, [])]
                bank = None
                if n in DRAIN:
                    inputs += [end.get((d, t)) for d in STEP[DRAIN[n]][4] if d != n]
                    open_banks = [(x, i) for i, x in enumerate(map(freed, range(BANKS))) if x is not None]
                    if not open_banks:
                        continue
                    x, bank = min(open_banks)
                    freed_at.append(x)
                if None in inputs or None in freed_at:
                    continue
                at = max([free[e]] + [x + SIGNAL for x in inputs + freed_at])
                able.append((at, n, t, bank, e == "act" and tab not in ("-", table)))
            if not able:
                continue
            first = min(c[0] for c in able)
            pick = max((c for c in able if c[0] <= first + WINDOW.get(e, 0)),
                       key=lambda c: rank[c[1], c[2]] - TABLE_BIAS * c[4] - (c[0] - first))
            if choice is None or pick[0] < choice[1][0]:
                choice = e, pick
        e, (at, n, t, bank, switch) = choice
        _, ns, land, tab, _ = STEP[n]
        left[e].remove((n, t))
        order.append((n, e, t))
        if e == "act" and tab != "-":
            table = tab
        free[e] = at + ns + TABLE_NS * switch
        end[n, t] = free[e]
        if land:
            dma_free = max(dma_free, free[e]) + land
            end[n, t] = dma_free + DMA_NS
        started[n, t] = at
        before = []
        for buf, readers in starts.get(n, []):
            before.append(owner.get((buf, t % SLOTS), ([], 0)))
            owner[buf, t % SLOTS] = (readers, t)
        if bank is not None:
            before.append(owner.get(bank, ([], 0)))
            owner[bank] = ([DRAIN[n]], t)
            bank_of[n, t] = bank
        previous[n, t] = [(r, bt) for readers, bt in before for r in readers]
    return order, bank_of, previous, started


WINDOW = {"act": 1500}
ORDER, BANK_OF, PREVIOUS, PLANNED = plan()


def build(nc, a, out):
    ctx = ExitStack()
    with ctx:
        def sb(name, shape, dt=F32):
            return ctx.enter_context(nc.sbuf_tensor(name, shape, dt))

        def sem(name):
            return ctx.enter_context(nc.semaphore(name))

        vdram = a["vdram"]
        bank = [ctx.enter_context(nc.psum_tensor(f"bank{i}", [P, 512], F32)) for i in range(8)]

        tab = sb("tab", [P, NCOL])
        rows = sb("rows", [P, NROW])
        up33 = sb("up33", [A + 1, D])
        evec0 = sb("evec0", [E0 + 1, 2 * A])
        idx0 = sb("idx0", [E0 + 1, B], I32)
        idx1 = sb("idx1", [P, B], I32)
        idx2 = sb("idx2", [E2, B], I32)
        gate = sb("gate", [P, NT])
        mask_u8 = sb("mask_u8", [P, NT * S], U8)
        mask_add = sb("mask_add", [P, NT, S])

        def col(name, lo=0, n=None):
            at, w = COL[name]
            return tab[:, at + lo:at + lo + (w if n is None else n)]

        def cvec(i, parts=P):
            at = COL["cvec"][0] + i
            return tab[0:parts, at:at + 1]

        def row(name, n=D):
            return rows[:, ROW[name]:ROW[name] + n]

        ident = col("ident")

        f0 = sb("f0", [E0 + 1, 4, B])
        oh0 = sb("oh0", [E0 + 1, 2, B])
        wsel = sb("wsel", [A, A, B])
        bias0 = sb("bias0", [A, B])
        ang = sb("ang", [P, 4, B])
        silu_t = sb("silu_t", [P, B])
        emb = sb("emb", [B, 2 * D])
        f2 = sb("f2", [E2, 4, B])
        eidx = sb("eidx", [1, B], I32)
        oh2 = sb("oh2", [E2, B])
        bi_sel = sb("bi_sel", [P, C, B])
        eps = sb("eps", [P, 2])

        x_in = sb("x_in", [P, NT, D])
        res = sb("res", [P, NT, D])
        resb = sb("resb", [P, NT, D])
        nrm = sb("nrm", [P, NT, D])
        hid = nrm[0:A]
        hid2 = resb[0:A + 1]
        xt = sb("xt", [P, NT, P])
        fm = sb("fm", [P, SLOTS, H, S])
        bn = sb("bn", [P, NT, 6])
        mv = sb("mv", [P, NT, 2])
        lnv = sb("lnv", [P, NT])
        rstd = sb("rstd", [P, NT])
        mx = sb("mx", [P, NT, H])
        rsum = sb("rsum", [P, NT, H])
        selv = sb("selv", [P, SLOTS, 3 * D])
        adav = sb("adav", [P, SLOTS, 2 * D])
        qkv = sb("qkv", [P, SLOTS, 3 * D])
        qkt = sb("qkt", [P, SLOTS, 2, HG, S])
        qbd = sb("qbd", [P, SLOTS, HG, NB, S])
        kex = sb("kex", [P, SLOTS, HG, H4, S])
        vbd = sb("vbd", [P, SLOTS, NB, HG, VW])
        sc = sb("sc", [P, SLOTS, H, S])
        vrep = sb("vrep", [P, SLOTS, NB, D])
        pt = sb("pt", [P, SLOTS, HG, P])
        cx = sb("cx", [P, SLOTS, D])
        cxt = sb("cxt", [P, SLOTS, P])
        hg = sb("hg", [P, SLOTS, C, P])
        experts0 = hg[0:E0 + 1, 0:2].rearrange("p k c q -> p (k c q)")
        evec2 = cxt[0:E2].rearrange("p k q -> p (k q)")
        ada_b = cx[0:B, 0:2].rearrange("p k q -> p (k q)")
        wexp = sb("wexp", [P, SLOTS, NB, 2 * FF])

        done = {name: sem("done_" + name) for name in STEP if STEP[name][0] != "sp"}
        loaded = {n: sem("loaded_" + n) for n in
                  ("xt", "x", "cvec", "tab0", "tab1", "tab3", "rows", "small0", "idx0", "idx1", "idx2", "up33", "ada_b", "evec2",
                   "gate", "mask")}
        landed = {n: [sem(f"landed_{n}_{k}") for k in range(SLOTS)] for n in TRANSFERS}
        eidx_ready = sem("eidx_ready")
        wl_landed = [sem("wl_even_landed"), sem("wl_odd_landed")]
        oh0_ready = sem("oh0_ready")
        oh2_ready = sem("oh2_ready")
        angle_ready = sem("angle_ready")
        silu_ready = sem("silu_ready")
        wsel_mm = sem("wsel_mm")
        bias0_mm = sem("bias0_mm")
        wsel_ready = sem("wsel_ready")
        emb_mm = sem("emb_mm")
        emb_ready = sem("emb_ready")
        bi_mm = sem("bi_mm")
        bi_ready = sem("bi_ready")
        preset = sem("preset")
        dchain = sem("dve_chain")
        achain = sem("act_chain")
        pchain = sem("pool_chain")
        stored = sem("stored")

        def arrived(eng, name, t):
            if name.startswith("wl"):
                piece = t * NB + int(name[-1])
                eng.wait_ge(wl_landed[piece % 2], 32 * (piece // 2 + 1))
                return
            eng.wait_ge(landed[name][t % SLOTS], 16 * TRANSFERS[name] * (t // SLOTS + 1))

        def reuse(eng, name, t):
            for reader, rt in PREVIOUS[name, t]:
                if STEP[reader][0] == "sp":
                    arrived(eng, reader, rt)
                else:
                    eng.wait_ge(done[reader], rt + 1)

        block = ctx.enter_context(nc.Block())

        @block.sync
        def _(sp):
            t1 = COL["wqkv1"][0]
            t3 = COL["wqkv3"][0]
            at = COL["cvec"][0]
            sp.dma_start(tab[:, at:at + 32], a["tab"][:, at:at + 32]).then_inc(loaded["cvec"], 16)
            sp.dma_start(experts0, a["experts0"]).then_inc(loaded["small0"], 16)
            sp.dma_start(xt[:].rearrange("p t s -> p (t s)"), a["xt"]).then_inc(loaded["xt"], 16)
            sp.dma_start(tab[:, 0:at], a["tab"][:, 0:at]).then_inc(loaded["tab0"], 16)
            sp.dma_start(tab[:, at + 32:t1], a["tab"][:, at + 32:t1]).then_inc(loaded["tab0"], 16)
            sp.dma_start(x_in[:], a["x"].rearrange("t p d -> p t d")).then_inc(loaded["x"], 16)
            sp.dma_start(rows[:], bass.AP(a["rows"].tensor, 0, [[0, P], [1, NROW]])).then_inc(loaded["rows"], 16)
            sp.dma_start(tab[:, t1:t3], a["tab"][:, t1:t3]).then_inc(loaded["tab1"], 16)
            sp.dma_start(mask_u8[:], a["mask"]).then_inc(loaded["mask"], 16)
            sp.dma_start(evec2, a["evec2"]).then_inc(loaded["evec2"], 16)
            sp.dma_start(gate[:], a["gate"]).then_inc(loaded["gate"], 16)
            sp.dma_start(tab[:, t3:NCOL], a["tab"][:, t3:NCOL]).then_inc(loaded["tab3"], 16)
            for name, engine, t in ORDER:
                if engine != "sp":
                    continue
                k = t % SLOTS
                layer = name[-1]
                if name != "store":
                    reuse(sp, name, t)
                    sig = landed[name][k] if name in landed else wl_landed[int(name[-1]) % 2]
                if name == "ada":
                    if t == 0:
                        sp.wait_ge(emb_ready, 1)
                    for_tokens = emb[t * NB:(t + 1) * NB, None, :].broadcast_to([NB, S, 2 * D])
                    sp.dma_start(adav[:, k, :], for_tokens).then_inc(sig, 16)
                elif name == "fs":
                    sp.dma_start(fm[:, k].rearrange("p h k -> p (h k)"), a["fside"][t]).then_inc(sig, 16)
                elif name in ("wl0", "wl1", "wl2", "wl3"):
                    b = int(name[-1])
                    if t == 0 and b < 2:
                        sp.wait_ge(eidx_ready, 1)
                    if b > 1:
                        arrived(sp, f"wl{b - 2}", t)
                    elif t > 0:
                        arrived(sp, f"wl{b + 2}", t - 1)
                    e = sp.value_load(eidx[0:1, t * NB + b:t * NB + b + 1], min_val=0, max_val=E2 - 1)
                    sp.dma_start(wexp[:, k, b, :],
                                 a["wexp"][bass.ds(e, 1), :, :].rearrange("o p n -> (o p) n")).then_inc(sig, 16)
                    sp.dma_start(selv[b * S:(b + 1) * S, k, :],
                                 a["eout2"][bass.ds(e, 1), :].broadcast_to([S, 3 * D])).then_inc(sig, 16)
                elif name in ("vw1", "vw3"):
                    sp.wait_ge(done["qkvb" + layer], t + 1)
                    sp.dma_start(vdram[k], qkv[:, k, 2 * D:3 * D]).then_inc(sig, 16)
                elif name in ("vr1", "vr3"):
                    arrived(sp, "vw" + layer, t)
                    for h in range(H4):
                        sp.dma_start(vrep[h * S:(h + 1) * S, k],
                                     vdram[k].rearrange("(b s) d -> s b d", b=NB)).then_inc(sig, 16)
                elif name == "store":
                    sp.wait_ge(done["gate"], t + 1)
                    sp.dma_start(out[t], nrm[:, t, :]).then_inc(stored, 16)
            sp.wait_ge(stored, 16 * NT)

        @block.tensor
        def _(pe):
            pe.wait_ge(loaded["small0"], 32)
            pe.wait_ge(oh0_ready, 1)
            for o in range(A):
                mm = pe.matmul(bank[3 + o // 16][0:A, (o % 16) * B:(o % 16 + 1) * B],
                               experts0[:, o * A:(o + 1) * A], oh0[:, 0, :], start=True, stop=True)
            mm.then_inc(wsel_mm, 1)
            pe.matmul(bank[5][0:A, 0:B], evec0[:, 0:A], oh0[:, 0, :], start=True, stop=False)
            pe.matmul(bank[5][0:A, 0:B], evec0[:, A:2 * A], oh0[:, 1, :], start=False, stop=True).then_inc(bias0_mm, 1)

            def once_emb():
                pe.wait_ge(silu_ready, 1)
                pe.wait_ge(loaded["tab0"], 32)
                pe.matmul(bank[6][0:B, 0:2 * D], silu_t[:], col("w_ada"), start=True, stop=True).then_inc(emb_mm, 1)

            def once_bi():
                pe.wait_ge(oh2_ready, 1)
                pe.wait_ge(loaded["evec2"], 16)
                for c in range(C):
                    mm = pe.matmul(bank[7][:, c * B:(c + 1) * B], evec2[:, c * P:(c + 1) * P], oh2[:],
                                   start=True, stop=True)
                mm.then_inc(bi_mm, 1)

            once_emb()
            once_bi()
            pe.wait_ge(wsel_ready, 1)
            pe.wait_ge(emb_ready, 1)
            pe.wait_ge(bi_ready, 1)
            pe.wait_ge(preset, 4)
            pe.wait_ge(loaded["up33"], 16)
            pe.wait_ge(loaded["xt"], 16)

            def transpose(dst, src):
                return pe.transpose(dst, src, ident)

            for name, engine, t in ORDER:
                if engine != "pe":
                    continue
                k = t % SLOTS
                ps = bank[BANK_OF[name, t]]
                reuse(pe, name, t)
                layer = name[-1]
                if name == "down":
                    mm = pe.matmul(ps[0:A, 0:P], col("down_wt"), xt[:, t, :], start=True, stop=True)
                elif name == "expert":
                    pe.wait_ge(done["gelu0"], t + 1)
                    for b in range(NB):
                        mm = pe.matmul(ps[0:A, b * S:(b + 1) * S], wsel[:, :, t * NB + b],
                                       hid[:, t, b * S:(b + 1) * S], start=True, stop=True)
                elif name == "up":
                    pe.wait_ge(done["ebias"], t + 1)
                    mm = pe.matmul(ps[:, 0:D], hid2[:, t, :], up33[:], start=True, stop=True)
                elif name in ("tr_b", "tr_d"):
                    pe.wait_ge(done["aff_b" if name == "tr_b" else "res2"], t + 1)
                    mm = transpose(ps[:, 0:P], res[:, t, :])
                elif name in ("tr_c", "tr_f", "tr_g"):
                    pe.wait_ge(done["norm_" + layer], t + 1)
                    mm = transpose(ps[:, 0:P], nrm[:, t, :])
                elif name in ("qkv1", "qkv3"):
                    pe.wait_ge(loaded["tab" + layer], 16)
                    pe.wait_ge(done["ev_b" if layer == "1" else "ev_f"], t + 1)
                    mm = pe.matmul(ps[:, 0:3 * D], xt[:, t, :], col("wqkv" + layer), start=True, stop=True)
                elif name in ("sc1", "sc3"):
                    pe.wait_ge(done["qbd" + layer], t + 1)
                    pe.wait_ge(done["kex" + layer], t + 1)
                    for g in range(HG):
                        mm = pe.matmul(ps[:, g * P:(g + 1) * P], qbd[:, k, g].rearrange("p b s -> p (b s)"),
                                       kex[:, k, g].rearrange("p h s -> p (h s)"), start=True, stop=True)
                elif name in ("pt1", "pt3"):
                    pe.wait_ge(done["exp" + layer], t + 1)
                    for g in range(HG):
                        mm = transpose(ps[:, g * P:(g + 1) * P],
                                       sc[:, k, g * H4:(g + 1) * H4, :].rearrange("p h s -> p (h s)"))
                elif name in ("ctx1", "ctx3"):
                    pe.wait_ge(done["evpt" + layer], t + 1)
                    pe.wait_ge(done["vbd" + layer], t + 1)
                    for g in range(HG):
                        for b in range(NB):
                            mm = pe.matmul(ps[b * S:(b + 1) * S, g * VW:(g + 1) * VW],
                                           pt[:, k, g, b * S:(b + 1) * S], vbd[:, k, b, g, :], start=True, stop=True,
                                           tile_position=(0, b * S))
                elif name in ("ct1", "ct3"):
                    pe.wait_ge(done["cn" + layer], t + 1)
                    mm = transpose(ps[:, 0:P], cx[:, k, :])
                elif name in ("wo1", "wo3"):
                    pe.wait_ge(done["evct" + layer], t + 1)
                    mm = pe.matmul(ps[:, 0:D], cxt[:, k, :], col("wo" + layer), start=True, stop=True)
                elif name in ("ff1", "ff3"):
                    pe.wait_ge(done["ev_c" if layer == "1" else "ev_g"], t + 1)
                    for c in range(C):
                        mm = pe.matmul(ps[:, c * P:(c + 1) * P], col("w1" + layer, c * P, P), xt[:, t, :],
                                       start=True, stop=True)
                elif name in ("fo1", "fo3"):
                    pe.wait_ge(done["act" + layer], t + 1)
                    for c in range(C):
                        mm = pe.matmul(ps[:, 0:D], hg[:, k, c, :], col("w2" + layer, c * D, D),
                                       start=(c == 0), stop=(c == C - 1))
                elif name == "e1":
                    pe.wait_ge(done["ev_d"], t + 1)
                    arrived(pe, "wl2", t)
                    arrived(pe, "wl3", t)
                    for b in range(NB):
                        mm = pe.matmul(ps[b * S:(b + 1) * S, :], xt[:, t, b * S:(b + 1) * S],
                                       wexp[:, k, b, 0:FF], start=True, stop=True, tile_position=(0, b * S))
                elif name == "et":
                    pe.wait_ge(done["eve1"], t + 1)
                    for c in range(C):
                        mm = transpose(ps[:, c * P:(c + 1) * P], pt[:, k, c, :])
                elif name == "e2":
                    pe.wait_ge(done["gelu2"], t + 1)
                    for c in range(C):
                        for b in range(NB):
                            mm = pe.matmul(ps[b * S:(b + 1) * S, 0:D], hg[:, k, c, b * S:(b + 1) * S],
                                           wexp[:, k, b, FF + c * D:FF + (c + 1) * D],
                                           start=(c == 0), stop=(c == C - 1), tile_position=(0, b * S))
                mm.then_inc(done[name], 1)

        @block.scalar
        def _(act):
            chain = [0]

            def link(ins):
                chain[0] += 1
                ins.then_inc(achain, 1)
                act.wait_ge(achain, chain[0])

            def spread(name, parts, n):
                return bass.AP(a[name].tensor, 0, [[0, parts], [1, n]])

            act.dma_start(idx0[:], spread("idx0", E0 + 1, B)).then_inc(loaded["idx0"], 16)
            act.dma_start(idx1[:], spread("idx1", P, B)).then_inc(loaded["idx1"], 16)
            act.dma_start(evec0[:], a["evec0"]).then_inc(loaded["small0"], 16)
            act.dma_start(idx2[:], spread("idx2", E2, B)).then_inc(loaded["idx2"], 16)
            act.dma_start(up33[:], a["up33"]).then_inc(loaded["up33"], 16)
            act.dma_start(ada_b, spread("ada_b", B, 2 * D)).then_inc(loaded["ada_b"], 16)
            act.wait_ge(angle_ready, 1)
            link(act.activation(silu_t[:], ang[:, 0, :], ACT.Sin))
            act.activation(silu_t[:], silu_t[:], ACT.Silu).then_inc(silu_ready, 1)
            act.wait_ge(preset, 4)
            act.wait_ge(loaded["tab0"], 32)
            table = ["none"]
            for name, engine, t in ORDER:
                if engine != "act":
                    continue
                k = t % SLOTS
                layer = name[-1]
                reuse(act, name, t)
                if name == "gelu0":
                    act.wait_ge(done["down"], t + 1)
                    table[0] = "gelu"
                    ins = act.activation(hid[:, t, :], bank[BANK_OF["down", t]][0:A, 0:P], ACT.Gelu, bias=cvec(C_DOWN_B, A))
                elif name.startswith("rstd"):
                    act.wait_ge(done["stat_" + layer], t + 1)
                    if table[0] != "ln":
                        act.preload_act_table_set("natural_log_exp_and_others")
                        table[0] = "ln"
                    link(act.activation(lnv[:, t:t + 1], mv[:, t, 1:2], ACT.Ln,
                                        bias=eps[:, 1:2] if layer == "e" else eps[:, 0:1]))
                    ins = act.activation(rstd[:, t:t + 1], lnv[:, t:t + 1], ACT.Exp, scale=-0.5)
                elif name in ("ev_b", "ev_d"):
                    act.wait_ge(done["tr_" + layer], t + 1)
                    ins = act.activation(xt[:, t, :], bank[BANK_OF["tr_" + layer, t]][:, 0:P], ACT.Copy)
                elif name in ("ev_c", "ev_f", "ev_g"):
                    act.wait_ge(done["tr_" + layer], t + 1)
                    s_, b_ = {"c": (C_G2, C_BETA2), "f": (C_G31, C_B31), "g": (C_G32, C_B32)}[layer]
                    ins = act.activation(xt[:, t, :], bank[BANK_OF["tr_" + layer, t]][:, 0:P], ACT.Identity, bias=cvec(b_), scale=cvec(s_))
                elif name in ("exp1", "exp3"):
                    act.wait_ge(done["sub" + layer], t + 1)
                    if table[0] != "ln":
                        act.preload_act_table_set("natural_log_exp_and_others")
                        table[0] = "ln"
                    ins = act.activation(sc[:, k], sc[:, k], ACT.Exp)
                elif name in ("evpt1", "evpt3"):
                    act.wait_ge(done["pt" + layer], t + 1)
                    ins = act.activation(pt[:, k].rearrange("p c q -> p (c q)"), bank[BANK_OF["pt" + layer, t]][:], ACT.Copy)
                elif name in ("evct1", "evct3"):
                    act.wait_ge(done["ct" + layer], t + 1)
                    ins = act.activation(cxt[:, k, :], bank[BANK_OF["ct" + layer, t]][:, 0:P], ACT.Copy)
                elif name in ("act1", "act3"):
                    act.wait_ge(done["ff" + layer], t + 1)
                    table[0] = "gelu"
                    for c in range(C):
                        ins = act.activation(hg[:, k, c, :], bank[BANK_OF["ff" + layer, t]][:, c * P:(c + 1) * P],
                                             ACT.Gelu_apprx_sigmoid if layer == "1" else ACT.Gelu,
                                             bias=cvec((C_B1_1 if layer == "1" else C_B1_3) + c))
                elif name == "eve1":
                    act.wait_ge(done["e1"], t + 1)
                    ins = act.activation(pt[:, k].rearrange("p c q -> p (c q)"), bank[BANK_OF["e1", t]][:], ACT.Copy)
                elif name == "gelu2":
                    act.wait_ge(done["eb"], t + 1)
                    table[0] = "gelu"
                    ins = act.activation(hg[:, k], hg[:, k], ACT.Gelu)
                ins.then_inc(done[name], 1)

        @block.vector
        def _(dve):
            chain = [0]

            def link(ins):
                chain[0] += 1
                ins.then_inc(dchain, 1)
                dve.wait_ge(dchain, chain[0])

            dve.memset(hid2[A:A + 1, :, :], 1.0).then_inc(preset, 1)
            dve.memset(eps[:, 0:1], EPS).then_inc(preset, 1)
            dve.memset(eps[:, 1:2], EPS2).then_inc(preset, 1)
            dve.wait_ge(loaded["idx0"], 16)
            dve.wait_ge(loaded["cvec"], 16)
            link(dve.tensor_copy(f0[:, 0, :], idx0[:]))
            link(dve.tensor_scalar(f0[:, 1, :], f0[:, 0, :], 0.0, float(E0 - 1), ALU.max, ALU.min))
            link(dve.tensor_tensor(f0[:, 2, :], f0[:, 0, :], f0[:, 1, :], ALU.not_equal))
            link(dve.tensor_scalar(f0[:, 3, :], f0[:, 2, :], float(E0 + 1), None, ALU.mult))
            link(dve.tensor_tensor(f0[:, 2, :], f0[:, 1, :], f0[:, 3, :], ALU.add))
            link(dve.tensor_scalar(f0[:, 3, :], f0[:, 2, :], float(E0), None, ALU.min))
            dve.tensor_scalar(oh0[:, 0, :], f0[:, 3, :], cvec(C_IOTA, E0 + 1), None, ALU.is_equal)
            dve.tensor_scalar(oh0[:, 1, :], f0[:, 1, :], cvec(C_IOTA, E0 + 1), None, ALU.is_equal).then_inc(oh0_ready, 1)
            dve.wait_ge(loaded["idx1"], 16)
            link(dve.tensor_copy(ang[:, 0, :], idx1[:]))
            link(dve.tensor_scalar(ang[:, 1, :], ang[:, 0, :], 40.0, cvec(C_FREQ), ALU.mult, ALU.mult))
            link(dve.tensor_scalar(ang[:, 2, :], ang[:, 1, :], cvec(C_PHASE), 1.0 / TWO_PI, ALU.add, ALU.mult))
            link(dve.tensor_scalar(ang[:, 3, :], ang[:, 2, :], ROUND, ROUND, ALU.add, ALU.subtract))
            link(dve.scalar_tensor_tensor(ang[:, 0, :], ang[:, 3, :], -PI_A, ang[:, 1, :], ALU.mult, ALU.add))
            link(dve.scalar_tensor_tensor(ang[:, 1, :], ang[:, 3, :], -PI_B, ang[:, 0, :], ALU.mult, ALU.add))
            link(dve.scalar_tensor_tensor(ang[:, 2, :], ang[:, 3, :], -PI_C, ang[:, 1, :], ALU.mult, ALU.add))
            link(dve.tensor_scalar(ang[:, 1, :], ang[:, 2, :], cvec(C_PHASE), 3.1415925, ALU.add, ALU.min))
            dve.tensor_scalar(ang[:, 0, :], ang[:, 1, :], -3.1415925, None, ALU.max).then_inc(angle_ready, 1)
            dve.wait_ge(loaded["idx2"], 16)
            link(dve.tensor_copy(f2[:, 0, :], idx2[:]))
            link(dve.tensor_scalar(f2[:, 1, :], f2[:, 0, :], 0.0, float(E2), ALU.is_lt, ALU.mult))
            link(dve.tensor_tensor(f2[:, 2, :], f2[:, 0, :], f2[:, 1, :], ALU.add))
            link(dve.tensor_scalar(f2[:, 3, :], f2[:, 2, :], 0.0, float(E2 - 1), ALU.max, ALU.min))
            dve.tensor_copy(eidx[:], f2[0:1, 3, :]).then_inc(eidx_ready, 1)
            dve.tensor_scalar(oh2[:], f2[:, 3, :], cvec(C_IOTA, E2), None, ALU.is_equal).then_inc(oh2_ready, 1)
            dve.wait_ge(wsel_mm, 1)
            for n in range(2):
                dve.tensor_copy(wsel[:, 16 * n:16 * n + 16, :].rearrange("a o b -> a (o b)"), bank[3 + n][0:A, :])
            dve.wait_ge(bias0_mm, 1)
            dve.tensor_copy(bias0[:], bank[5][0:A, 0:B]).then_inc(wsel_ready, 1)
            dve.wait_ge(emb_mm, 1)
            dve.wait_ge(loaded["ada_b"], 16)
            dve.tensor_tensor(emb[:], bank[6][0:B, 0:2 * D], ada_b, ALU.add).then_inc(dchain, 1)
            chain[0] += 1
            dve.wait_ge(dchain, chain[0])
            dve.tensor_scalar(emb[:, 0:D], emb[:, 0:D], 1.0, None, ALU.add).then_inc(emb_ready, 1)
            dve.wait_ge(bi_mm, 1)
            dve.tensor_copy(bi_sel[:].rearrange("p c b -> p (c b)"), bank[7][:, 0:C * B]).then_inc(bi_ready, 1)
            dve.wait_ge(wsel_ready, 1)
            dve.wait_ge(preset, 4)
            dve.wait_ge(loaded["x"], 16)
            dve.wait_ge(loaded["rows"], 16)
            dve.wait_ge(loaded["gate"], 16)

            prev_norm = {"a": "res0", "b": "aff_a", "c": "res1", "e": "res3", "f": "aff_e", "g": "res4"}
            for name, engine, t in ORDER:
                if engine != "dve":
                    continue
                k = t % SLOTS
                layer = name[-1]
                reuse(dve, name, t)
                if name == "ebias":
                    dve.wait_ge(done["expert"], t + 1)
                    ins = dve.tensor_tensor(
                        hid2[0:A, t, :].rearrange("o (b s) -> o b s", b=NB),
                        bank[BANK_OF["expert", t]][0:A, 0:P].rearrange("o (b s) -> o b s", b=NB),
                        bias0[:, t * NB:(t + 1) * NB, None].broadcast_to([A, NB, S]), ALU.add)
                elif name == "res0":
                    dve.wait_ge(done["up"], t + 1)
                    ins = dve.tensor_tensor(res[:, t, :], bank[BANK_OF["up", t]][:, 0:D], x_in[:, t, :], ALU.add)
                elif name.startswith("stat"):
                    dve.wait_ge(done[prev_norm[layer]], t + 1)
                    link(dve.bn_stats(bn[:, t, :], res[:, t, :]))
                    ins = dve.bn_aggr(mv[:, t, :], bn[:, t, :])
                elif name.startswith("norm"):
                    dve.wait_ge(done["rstd_" + layer], t + 1)
                    ins = dve.tensor_scalar(nrm[:, t, :], res[:, t, :], mv[:, t, 0:1], rstd[:, t:t + 1],
                                            ALU.subtract, ALU.mult)
                elif name == "aff_b":
                    dve.wait_ge(done["norm_b"], t + 1)
                    arrived(dve, "ada", t)
                    link(dve.tensor_tensor(res[:, t, :], nrm[:, t, :], adav[:, k, 0:D], ALU.mult))
                    ins = dve.tensor_tensor(res[:, t, :], res[:, t, :], adav[:, k, D:2 * D], ALU.add)
                elif name in ("qkvb1", "qkvb3"):
                    dve.wait_ge(done["qkv" + layer], t + 1)
                    ins = dve.tensor_tensor(qkv[:, k, :], bank[BANK_OF["qkv" + layer, t]][:, 0:3 * D],
                                            row("bqkv" + layer, 3 * D), ALU.add)
                elif name in ("qkt1", "qkt3"):
                    dve.wait_ge(done["qkvb" + layer], t + 1)
                    ins = dve.transpose(qkt[:, k].rearrange("p j g s -> p (j g s)"), qkv[:, k, 0:2 * D])
                elif name in ("kex1", "kex3"):
                    dve.wait_ge(done["qkt" + layer], t + 1)
                    ins = dve.tensor_tensor(kex[:, k], qkt[:, k, 1, :, None, :].broadcast_to([P, HG, H4, S]),
                                            col("head_mask")[:, None, :, None].broadcast_to([P, HG, H4, S]), ALU.mult)
                elif name in ("vbd1", "vbd3"):
                    arrived(dve, "vr" + layer, t)
                    n = NB * HG
                    ins = dve.tensor_tensor(
                        vbd[:, k].rearrange("p b g w -> p (b g) w")[:, :, 0:H4 * DH].rearrange(
                            "p n (h d) -> p n h d", h=H4),
                        vrep[:, k].rearrange("p b (g h d) -> p (b g) h d", g=HG, h=H4),
                        col("seq_mask")[:, None, :, None].broadcast_to([P, n, H4, DH]), ALU.mult)
                elif name in ("sb1", "sb3"):
                    dve.wait_ge(done["sc" + layer], t + 1)
                    if layer == "1":
                        dve.wait_ge(done["mask1"], t + 1)
                        bias = fm[:, k]
                    else:
                        bias = col("causal")[:, None, :].broadcast_to([P, H, S])
                    ins = dve.tensor_tensor(sc[:, k], bank[BANK_OF["sc" + layer, t]][:].rearrange("p (h s) -> p h s", h=H), bias, ALU.add)
                elif name in ("mx1", "mx3"):
                    dve.wait_ge(done["sb" + layer], t + 1)
                    ins = dve.tensor_reduce(mx[:, t, :], sc[:, k], AX.X, ALU.max)
                elif name in ("cn1", "cn3"):
                    dve.wait_ge(done["ctx" + layer], t + 1)
                    p4 = bank[BANK_OF["ctx" + layer, t]][:, 0:HG * VW].rearrange("p (g w) -> p g w", g=HG)
                    link(dve.reciprocal(rsum[:, t, :].rearrange("p (g h) -> p g h", g=HG), p4[:, :, H4 * DH:VW]))
                    ins = dve.tensor_tensor(
                        cx[:, k, :].rearrange("p (g h d) -> p g h d", g=HG, h=H4),
                        p4[:, :, 0:H4 * DH].rearrange("p g (h d) -> p g h d", h=H4),
                        rsum[:, t, :].rearrange("p (g h) -> p g h", g=HG)[:, :, :, None].broadcast_to(
                            [P, HG, H4, DH]), ALU.mult)
                elif name in ("res1", "res4"):
                    l_ = "1" if name == "res1" else "3"
                    dve.wait_ge(done["wo" + l_], t + 1)
                    dve.wait_ge(done["xbo" + l_], t + 1)
                    ins = dve.tensor_tensor(res[:, t, :], bank[BANK_OF["wo" + l_, t]][:, 0:D],
                                            resb[:, t, :], ALU.add)
                elif name == "res2":
                    dve.wait_ge(done["fo1"], t + 1)
                    dve.wait_ge(done["xb21"], t + 1)
                    ins = dve.tensor_tensor(res[:, t, :], bank[BANK_OF["fo1", t]][:, 0:D], resb[:, t, :], ALU.add)
                elif name == "eb":
                    dve.wait_ge(done["et"], t + 1)
                    ins = dve.tensor_tensor(
                        hg[:, k].rearrange("p c (b s) -> p c b s", b=NB),
                        bank[BANK_OF["et", t]][:].rearrange("p (c b s) -> p c b s", c=C, b=NB),
                        bi_sel[:, :, t * NB:(t + 1) * NB, None].broadcast_to([P, C, NB, S]), ALU.add)
                elif name == "res3":
                    dve.wait_ge(done["e2"], t + 1)
                    dve.wait_ge(done["xbo2"], t + 1)
                    ins = dve.tensor_tensor(res[:, t, :], bank[BANK_OF["e2", t]][:, 0:D], resb[:, t, :], ALU.add)
                elif name == "res5":
                    dve.wait_ge(done["fo3"], t + 1)
                    dve.wait_ge(done["xb23"], t + 1)
                    ins = dve.tensor_tensor(resb[:, t, :], bank[BANK_OF["fo3", t]][:, 0:D], resb[:, t, :], ALU.add)
                elif name == "gate":
                    dve.wait_ge(done["res5"], t + 1)
                    ins = dve.scalar_tensor_tensor(nrm[:, t, :], resb[:, t, :], gate[:, t:t + 1], x_in[:, t, :],
                                                   ALU.mult, ALU.add)
                ins.then_inc(done[name], 1)

        @block.gpsimd
        def _(pool):
            chain = [0]

            def link(ins):
                chain[0] += 1
                ins.then_inc(pchain, 1)
                pool.wait_ge(pchain, chain[0])

            pool.wait_ge(loaded["tab0"], 32)
            pool.tensor_copy(
                vbd[:].rearrange("p k b g w -> p (k b g) w")[:, :, H4 * DH:VW],
                col("seq_mask")[:, None, :].broadcast_to([P, SLOTS * NB * HG, H4])).then_inc(preset, 1)
            pool.wait_ge(loaded["mask"], 16)
            link(pool.tensor_scalar(mask_add[:].rearrange("p t k -> p (t k)"), mask_u8[:], NEG, None, ALU.mult))
            pool.wait_ge(loaded["rows"], 16)
            for name, engine, t in ORDER:
                if engine != "pool":
                    continue
                k = t % SLOTS
                layer = name[-1]
                reuse(pool, name, t)
                if name == "aff_a":
                    pool.wait_ge(done["norm_a"], t + 1)
                    link(pool.tensor_tensor(res[:, t, :], nrm[:, t, :], row("g0"), ALU.mult))
                    ins = pool.tensor_tensor(res[:, t, :], res[:, t, :], row("be0"), ALU.add)
                elif name == "aff_e":
                    pool.wait_ge(done["norm_e"], t + 1)
                    link(pool.tensor_tensor(res[:, t, :], nrm[:, t, :], selv[:, k, D:2 * D], ALU.mult))
                    link(pool.tensor_tensor(res[:, t, :], res[:, t, :], selv[:, k, 2 * D:3 * D], ALU.add))
                    ins = pool.tensor_copy(x_in[:, t, :], res[:, t, :])
                elif name in ("xbo1", "xbo3"):
                    pool.wait_ge(done["aff_b" if layer == "1" else "aff_e"], t + 1)
                    ins = pool.tensor_tensor(resb[:, t, :], res[:, t, :], row("bo" + layer), ALU.add)
                elif name == "mask1":
                    arrived(pool, "fs", t)
                    ins = pool.tensor_tensor(fm[:, k], fm[:, k], mask_add[:, t, None, :].broadcast_to([P, H, S]),
                                             ALU.add)
                elif name in ("qbd1", "qbd3"):
                    pool.wait_ge(done["qkt" + layer], t + 1)
                    at = COL["cvec"][0] + 20
                    ins = pool.tensor_tensor(qbd[:, k], qkt[:, k, 0, :, None, :].broadcast_to([P, HG, NB, S]),
                                             tab[:, None, at:at + NB, None].broadcast_to([P, HG, NB, S]), ALU.mult)
                elif name in ("sub1", "sub3"):
                    pool.wait_ge(done["mx" + layer], t + 1)
                    ins = pool.tensor_tensor(sc[:, k], sc[:, k], mx[:, t, :, None].broadcast_to([P, H, S]),
                                             ALU.subtract)
                elif name == "xb21":
                    pool.wait_ge(done["res1"], t + 1)
                    ins = pool.tensor_tensor(resb[:, t, :], res[:, t, :], row("b21"), ALU.add)
                elif name == "xbo2":
                    pool.wait_ge(done["res2"], t + 1)
                    arrived(pool, "wl2", t)
                    arrived(pool, "wl3", t)
                    ins = pool.tensor_tensor(resb[:, t, :], res[:, t, :], selv[:, k, 0:D], ALU.add)
                elif name == "xb23":
                    pool.wait_ge(done["res4"], t + 1)
                    link(pool.tensor_tensor(resb[:, t, :], res[:, t, :], row("b23"), ALU.add))
                    ins = pool.tensor_tensor(resb[:, t, :], resb[:, t, :], x_in[:, t, :], ALU.subtract)
                ins.then_inc(done[name], 1)


def kernel(**inputs):
    import numpy as np
    import concourse.bacc as _bacc
    from concourse import mybir as _mybir
    from concourse.bass_utils import run_bass_kernel_spmd as _run

    v = {n: np.asarray(a) for n, a in inputs.items()}
    f = np.float32

    def cols(a):
        return np.ascontiguousarray(a.reshape(-1, P).T)

    def chunks(w):
        return w.reshape(C, P, -1).transpose(1, 0, 2).reshape(P, -1)

    p = np.arange(P)
    cvec = np.zeros((P, 32), f)
    cvec[0:A, C_DOWN_B] = v["L0_cond_down_b"]
    half = D // 2
    freqs = np.exp(np.arange(half, dtype=f) * f(-math.log(10000.0) / (half - 1))).astype(f)
    cvec[:, C_FREQ] = np.concatenate([freqs, freqs])
    cvec[half:, C_PHASE] = math.pi / 2
    cvec[:, C_IOTA] = p
    for i, n in ((C_BV1, "L1_cond_bv"), (C_G2, "L1_cond_g2"), (C_BETA2, "L1_cond_beta2"), (C_BV3, "L3_cond_bv"),
                 (C_G31, "L3_cond_gamma1"), (C_B31, "L3_cond_beta1"), (C_G32, "L3_cond_gamma2"),
                 (C_B32, "L3_cond_beta2")):
        cvec[:, i] = v[n]
    cvec[:, C_B1_1:C_B1_1 + C] = cols(v["L1_cond_b1"])
    cvec[:, C_B1_3:C_B1_3 + C] = cols(v["L3_cond_b1"])
    seq_mask = (p[:, None] // S == np.arange(NB)[None, :]).astype(f)
    cvec[:, 20:20 + NB] = seq_mask * f(1.0 / math.sqrt(DH))
    parts = {
        "ident": np.eye(P, dtype=f), "down_wt": v["L0_cond_down_W"].T, "seq_mask": seq_mask,
        "head_mask": ((p[:, None] % S) // DH == np.arange(H4)[None, :]).astype(f), "cvec": cvec,
        "w_ada": v["L1_cond_W_ada"],
        "causal": np.where(np.arange(S)[None, :] <= (p % S)[:, None], 0.0, NEG).astype(f),
    }
    for l in "13":
        w = {n: v[f"L{l}_cond_{n}"] for n in ("Wq", "Wk", "Wv", "Wo", "W1", "W2")}
        parts.update({"wqkv" + l: np.concatenate([w["Wq"], w["Wk"], w["Wv"]], 1), "wo" + l: w["Wo"],
                      "w1" + l: w["W1"], "w2" + l: chunks(w["W2"])})
    tab = np.concatenate([parts[n] for n, _ in COLS], 1)
    rows = np.concatenate([v[n] for n in (
        "L0_cond_ln_gamma", "L0_cond_ln_beta", "L1_cond_bq", "L1_cond_bk", "L1_cond_bv", "L1_cond_bo", "L1_cond_b2",
        "L3_cond_bq", "L3_cond_bk", "L3_cond_bv", "L3_cond_bo", "L3_cond_b2")])
    experts0 = np.concatenate([v["L0_cond_expert_W"].reshape(E0, A * A), np.eye(A, dtype=f).reshape(1, A * A)])
    evec0 = np.concatenate([np.concatenate([v["L0_cond_expert_b"], v["L0_cond_domain_emb"]], 1),
                            np.zeros((1, 2 * A), f)])
    wi = v["L2_cond_Wi"]
    wo = v["L2_cond_Wo"].reshape(E2, C, P, D).transpose(0, 2, 1, 3).reshape(E2, P, C * D)
    laid = {
        "x": v["x"].reshape(NT, P, D),
        "xt": v["x"].reshape(NT * P, D).T,
        "tab": tab, "rows": rows, "experts0": experts0, "evec0": evec0,
        "up33": np.concatenate([v["L0_cond_up_W"].T, v["L0_cond_up_b"][None]]),
        "ada_b": v["L1_cond_b_ada"],
        "evec2": v["L2_cond_bi"],
        "eout2": np.concatenate([v["L2_cond_" + n] for n in ("bo", "gamma", "beta")], 1),
        "wexp": np.concatenate([wi, wo], 2),
        "fside": v["fside_Bx16xSxS_0"].reshape(NT, NB, H, S, S).transpose(0, 1, 3, 2, 4).reshape(NT, P, H * S),
        "mask": v["mask_Bx1xSxS_bk0"].reshape(NT, P, S).transpose(1, 0, 2).reshape(P, NT * S),
        "idx0": v["itok_B_0_15"], "idx1": v["itok_B_34_63"], "idx2": v["itok_B_0_7"],
        "gate": np.repeat(v["condB_gatescore"], S).reshape(NT, P).T,
    }
    nc = _bacc.Bacc("TRN2", target_bir_lowering=False, num_devices=1)
    arrays, aps = {}, {}
    for name, x in laid.items():
        x = np.ascontiguousarray(x)
        arrays[f"in_{name}"] = x
        aps[name] = nc.dram_tensor(f"in_{name}", x.shape, _mybir.dt.from_np(x.dtype), kind="ExternalInput").ap()
    out = nc.dram_tensor("out_0", (NT, P, D), _mybir.dt.float32, kind="ExternalOutput").ap()
    aps["vdram"] = nc.dram_tensor("vdram", (SLOTS, P, D), _mybir.dt.float32, kind="Internal").ap()
    build(nc, aps, out)
    r = _run(nc, [arrays], core_ids=[0])
    return r.results[0]["out_0"].reshape(B, S, D)
```

```python
import math
from contextlib import ExitStack

import concourse.bass as bass
from concourse import mybir

F32 = mybir.dt.float32
I32 = mybir.dt.int32
U8 = mybir.dt.uint8
BF16 = mybir.dt.bfloat16
ALU = mybir.AluOpType
ACT = mybir.ActivationFunctionType
AX = mybir.AxisListType

P = 128
B, S, D = 32, 32, 128
NB = P // S
NT = B // NB
H, DH = 16, 8
HG = 4
H4 = H // HG
A = 32
E0, E2 = 16, 8
FF = 512
C = FF // P
VW = H4 * DH + H4
SLOTS = 3
W_SLOTS = 5
EPS = 1e-5
EPS2 = 1e-12
NEG = -1e30
TWO_PI = 2 * math.pi
PI_A = 6.28125
PI_B = 0.00193500518798828125
PI_C = TWO_PI - PI_A - PI_B
ROUND = 1.5 * 2.0**23

WARM_UP = 36

COLS = [
    ("ident", P), ("down_wt", A), ("seq_mask", NB), ("head_mask", H4), ("cvec", 32),
    ("w_ada", 2 * D), ("causal", S),
    ("wqkv1", 3 * D), ("wo1", D), ("w11", FF), ("w21", FF),
    ("wqkv3", 3 * D), ("wo3", D), ("w13", FF), ("w23", FF),
]
COL = {}
_at = 0
for _n, _w in COLS:
    COL[_n] = (_at, _w)
    _at += _w
NCOL = _at
(C_DOWN_B, C_FREQ, C_PHASE, C_IOTA, C_BV1, C_G2, C_BETA2, C_BV3, C_G31, C_B31, C_G32, C_B32) = range(12)
C_B1_1, C_B1_3 = 12, 16
ROWS = ["g0", "be0", "bqkv1", "bk1", "bv1", "bo1", "b21", "bqkv3", "bk3", "bv3", "bo3", "b23"]
ROW = {n: i * D for i, n in enumerate(ROWS)}
NROW = len(ROWS) * D

STEPS = """
w_oh0  dve  1600 -    ;
w_ang  dve  2015 -    ;
w_oh2  dve  1150 -    ;
w_pre  pool 1000 -    ;
w_neg  pool 150  -    ;
w_silu act  2000 silu ; w_ang
w_sel  pe   2100 -    ; w_oh0
w_selc dve  1300 -    ; w_sel
w_emb  pe   860  -    ; w_silu w_selc
w_embc dve  550  -    ; w_emb
w_bi   pe   1100 -    ; w_oh2 w_embc
w_bic  dve  190  -    ; w_bi
ada    sp   100/600 -    ; w_embc@0
fs     sp   100/1000 -    ;
wl0    sp   500/2100 -    ; wl2@-1 w_oh2@0
wl1    sp   500/2100 -    ; wl3@-1 w_oh2@0
wl2    sp   500/2100 -    ; wl0
wl3    sp   500/2100 -    ; wl1
down   pe   426  -    ;
gelu0  act  260  gelu ; down
expert pe   424  -    ; gelu0 w_selc@0
ebias  dve  202  -    ; expert
up     pe   426  -    ; ebias
res0   dve  202  -    ; up
stat_a dve  404  -    ; res0
rstd_a act  585  ln   ; stat_a
norm_a dve  256  -    ; rstd_a
aff_a  pool 936  -    ; norm_a
stat_b dve  404  -    ; aff_a
rstd_b act  585  ln   ; stat_b
norm_b dve  256  -    ; rstd_b
aff_b  dve  531  -    ; norm_b ada
tr_b   pe   134  -    ; aff_b
ev_b   act  158  -    ; tr_b
xbo1   pool 417  -    ; aff_b
qkv1   pe   700  -    ; ev_b
qkvb1  dve  470  -    ; qkv1
vw1    sp   100/300  -    ; qkvb1
vr1    sp   400/1200 -    ; vw1
qkt1   dve  335  -    ; qkvb1
qbd1   pool 1001 -    ; qkt1
kex1   pool 1001 -    ; qkt1
sc1    pe   1120 -    ; qbd1 kex1 w_neg@0
sb1    dve  602  -    ; sc1 fs
mx1    dve  602  -    ; sb1
sub1   pool 1001 -    ; mx1
exp1   act  520  ln   ; sub1
pt1    pe   428  -    ; exp1
evpt1  act  478  -    ; pt1
vbd1   pool 1001 -    ; vr1
ctx1   pe   500  -    ; evpt1 vbd1 w_pre@0
cn1    dve  494  -    ; ctx1
ct1    pe   134  -    ; cn1
evct1  act  158  -    ; ct1
wo1    pe   242  -    ; evct1
res1   dve  202  -    ; wo1 xbo1
stat_c dve  404  -    ; res1
xb21   pool 417  -    ; res1
rstd_c act  585  ln   ; stat_c
norm_c dve  256  -    ; rstd_c
tr_c   pe   134  -    ; norm_c
ev_c   dve  344  -    ; tr_c
ff1    pe   866  -    ; ev_c
act1   act  690  gas  ; ff1
fo1    pe   866  -    ; act1
res2   dve  202  -    ; fo1 xb21
tr_d   pe   134  -    ; res2
ev_d   act  158  -    ; tr_d
xbo2   pool 417  -    ; res2 wl2 wl3
e1     pe   920  -    ; ev_d wl2 wl3
eve1   dve  602  -    ; e1
et     pe   428  -    ; eve1
eb     dve  602  -    ; et w_bic@0
gelu2  act  490  gelu ; eb
e2     pe   1110 -    ; gelu2
res3   dve  202  -    ; e2 xbo2
stat_e dve  404  -    ; res3
rstd_e act  585  ln   ; stat_e
norm_e dve  256  -    ; rstd_e
aff_e  pool 936  -    ; norm_e
stat_f dve  404  -    ; aff_e
rstd_f act  585  ln   ; stat_f
norm_f dve  256  -    ; rstd_f
tr_f   pe   134  -    ; norm_f
ev_f   dve  344  -    ; tr_f
xbo3   pool 417  -    ; aff_e
qkv3   pe   650  -    ; ev_f
qkvb3  dve  470  -    ; qkv3
vw3    sp   100/300  -    ; qkvb3
vr3    sp   400/1200 -    ; vw3
qkt3   dve  335  -    ; qkvb3
qbd3   pool 1001 -    ; qkt3
kex3   dve  602  -    ; qkt3
sc3    pe   1120 -    ; qbd3 kex3
mx3    dve  602  -    ; sc3
sub3   dve  602  -    ; mx3
exp3   act  520  ln   ; sub3
pt3    pe   428  -    ; exp3
evpt3  act  478  -    ; pt3
vbd3   pool 1001 -    ; vr3
ctx3   pe   520  -    ; evpt3 vbd3
cn3    dve  494  -    ; ctx3
ct3    pe   134  -    ; cn3
evct3  act  158  -    ; ct3
wo3    pe   242  -    ; evct3
res4   dve  202  -    ; wo3 xbo3
stat_g dve  404  -    ; res4
xb23   pool 936  -    ; res4
rstd_g act  585  ln   ; stat_g
norm_g dve  256  -    ; rstd_g
tr_g   pe   134  -    ; norm_g
ev_g   dve  344  -    ; tr_g
ff3    pe   900  -    ; ev_g
act3   act  690  gelu ; ff3
fo3    pe   900  -    ; act3
res5   dve  202  -    ; fo3 xb23
gate   dve  263  -    ; res5
store  sp   100/300  -    ; gate
"""
STEP = {}
for _line in STEPS.strip().splitlines():
    _head, _deps = _line.split(";")
    _name, _engine, _ns, _table = _head.split()
    _ns = [int(x) for x in _ns.split("/")]
    STEP[_name] = (_engine, _ns[0], _ns[-1] if len(_ns) > 1 else 0, _table, _deps.split())

DRAIN = {"down": "gelu0", "expert": "ebias", "up": "res0", "tr_b": "ev_b", "qkv1": "qkvb1", "sc1": "sb1",
         "pt1": "evpt1", "ctx1": "cn1", "ct1": "evct1", "wo1": "res1", "tr_c": "ev_c", "ff1": "act1",
         "fo1": "res2", "tr_d": "ev_d", "e1": "eve1", "et": "eb", "e2": "res3", "tr_f": "ev_f",
         "qkv3": "qkvb3", "sc3": "sub3", "pt3": "evpt3", "ctx3": "cn3", "ct3": "evct3", "wo3": "res4",
         "tr_g": "ev_g", "ff3": "act3", "fo3": "res5"}
SLOT_USES = {
    "adav": [("ada", ["aff_b"])],
    "fm": [("fs", ["sb1"])],
    "wexp02": [("wl0", ["e2"])],
    "wexp13": [("wl1", ["e2"])],
    "qkv": [("qkvb1", ["qkt1", "vw1"]), ("qkvb3", ["qkt3", "vw3"])],
    "vdram": [("vw1", ["vr1"]), ("vw3", ["vr3"])],
    "qkt": [("qkt1", ["qbd1", "kex1"]), ("qkt3", ["qbd3", "kex3"])],
    "qbd": [("qbd1", ["sc1"]), ("qbd3", ["sc3"])],
    "kex": [("kex1", ["sc1"]), ("kex3", ["sc3"])],
    "vrep": [("vr1", ["vbd1"]), ("vr3", ["vbd3"])],
    "vbd": [("vbd1", ["ctx1"]), ("vbd3", ["ctx3"])],
    "sc": [("sb1", ["pt1"]), ("sub3", ["pt3"])],
    "pt": [("evpt1", ["ctx1"]), ("eve1", ["et"]), ("evpt3", ["ctx3"])],
    "cx": [("cn1", ["ct1"]), ("cn3", ["ct3"])],
    "cxt": [("evct1", ["wo1"]), ("evct3", ["wo3"])],
    "hg": [("act1", ["fo1"]), ("eb", ["e2"]), ("act3", ["fo3"])],
}
TRANSFERS = {"ada": 1, "fs": 1,  "vw1": 1, "vr1": H4, "vw3": 1, "vr3": H4}
RINGS = {"wexp02": W_SLOTS, "wexp13": W_SLOTS}
BANKS = 8
ONCE = [n for n in STEP if n.startswith("w_")]
BANK_SEL, BANK_ONCE = (5, 6), 7
ONCE_BANKS = {5: "w_selc", 6: "w_selc", 7: "w_bic"}
LOADED_NS = {"w_oh0": 3200, "w_ang": 3400, "w_oh2": 4500, "w_pre": 6500, "w_neg": 11000, "w_sel": 5200, "down": 6500,
             "res0": 9000, "aff_a": 10000, "w_emb": 9500, "w_bi": 14500, "wl0": 14500, "wl1": 14500,
             "qkv1": 14000}
PRESETS = 3
SIGNAL = 260
DMA_NS = 2000
TABLE_NS = 1300
TABLE_BIAS = 5000
TILE_NS = 2500
START_NS = 5000


def ring(buf):
    return RINGS.get(buf, SLOTS)


def plan():
    succ = {n: [] for n in STEP}
    for n, (_, _, _, _, deps) in STEP.items():
        for d in deps:
            if not d.endswith("@-1"):
                succ[d.removesuffix("@0")].append(n)
    tail = {}
    for n in reversed(list(STEP)):
        _, ns, land, _, _ = STEP[n]
        tail[n] = ns + land + SIGNAL + max([tail[m] for m in succ[n]], default=0)
    starts = {}
    for buf, uses in SLOT_USES.items():
        for writer, readers in uses:
            starts.setdefault(writer, []).append((buf, readers))
    rank = {(n, t): tail[n] - TILE_NS * t for n in STEP for t in range(NT)}
    end = {}
    owner = {b: ([reader], 0) for b, reader in ONCE_BANKS.items()}
    bank_of, previous, started, order = {}, {}, {}, []
    left = {e: [(n, t) for n in STEP for t in range(1 if n in ONCE else NT) if STEP[n][0] == e] for e in
            ("pe", "dve", "act", "pool", "sp")}
    free = {e: 0 for e in left}
    free["sp"] = START_NS
    table = None
    dma_free = 0

    def freed(what):
        if what not in owner:
            return 0
        readers, t = owner[what]
        times = [end.get((r, t)) for r in readers]
        return None if None in times else max(times)

    while any(left.values()):
        choice = None
        for e, steps in left.items():
            able, seen = [], set()
            for n, t in steps:
                if n in seen:
                    continue
                seen.add(n)
                _, ns, land, tab, deps = STEP[n]
                inputs = [end.get((d, t)) for d in deps if "@" not in d]
                inputs += [end.get((d[:-3], t - 1)) for d in deps if d.endswith("@-1") and t > 0]
                inputs += [end.get((d[:-2], 0)) for d in deps if d.endswith("@0")]
                freed_at = [freed((buf, t % ring(buf))) for buf, _ in starts.get(n, [])]
                bank = None
                if n in DRAIN:
                    inputs += [end.get((d, t)) for d in STEP[DRAIN[n]][4]
                               if d != n and "@" not in d and n not in STEP[d][4]]
                    open_banks = [(x, i) for i, x in enumerate(map(freed, range(BANKS))) if x is not None]
                    if not open_banks:
                        continue
                    x, bank = min(open_banks)
                    freed_at.append(x)
                if None in inputs or None in freed_at:
                    continue
                at = max([free[e], LOADED_NS.get(n, 0)] + [x + SIGNAL for x in inputs + freed_at])
                able.append((at, n, t, bank, e == "act" and tab not in ("-", table)))
            if not able:
                continue
            first = min(c[0] for c in able)
            pick = max((c for c in able if c[0] <= first + WINDOW.get(e, 0)),
                       key=lambda c: rank[c[1], c[2]] - TABLE_BIAS * c[4] - (c[0] - first))
            if choice is None or pick[0] < choice[1][0]:
                choice = e, pick
        e, (at, n, t, bank, switch) = choice
        _, ns, land, tab, _ = STEP[n]
        left[e].remove((n, t))
        order.append((n, e, t))
        if e == "act" and tab != "-":
            table = tab
        free[e] = at + ns + TABLE_NS * switch
        end[n, t] = free[e]
        if land:
            dma_free = max(dma_free, free[e]) + land
            end[n, t] = dma_free + DMA_NS
        started[n, t] = at
        before = []
        for buf, readers in starts.get(n, []):
            before.append(owner.get((buf, t % ring(buf)), ([], 0)))
            owner[buf, t % ring(buf)] = (readers, t)
        if bank is not None:
            before.append(owner.get(bank, ([], 0)))
            owner[bank] = ([DRAIN[n]], t)
            bank_of[n, t] = bank
        previous[n, t] = [(r, bt) for readers, bt in before for r in readers]
    return order, bank_of, previous, started


WINDOW = {"act": 1500, "dve": 200, "pe": 50}
ORDER, BANK_OF, PREVIOUS, PLANNED = plan()


def build(nc, a, out):
    ctx = ExitStack()
    with ctx:
        def sb(name, shape, dt=F32):
            return ctx.enter_context(nc.sbuf_tensor(name, shape, dt))

        def sem(name):
            return ctx.enter_context(nc.semaphore(name))

        vdram = a["vdram"]
        bank = [ctx.enter_context(nc.psum_tensor(f"bank{i}", [P, 512], F32)) for i in range(8)]

        tab = sb("tab", [P, NCOL])
        rows = sb("rows", [P, NROW])
        up33 = sb("up33", [A + 1, D])
        idx0 = sb("idx0", [E0 + 1, B], I32)
        idx1 = sb("idx1", [P, B], I32)
        idx2 = sb("idx2", [E2, B], I32)
        gate = sb("gate", [P, NT])
        mask_u8 = sb("mask_u8", [P, NT * S], U8)
        mask_neg = sb("mask_neg", [P, NT, S], BF16)
        causal_neg = sb("causal_neg", [P, S], BF16)
        ident_bf = sb("ident_bf", [P, P], BF16)
        idle_bf = sb("idle_bf", [P, P], BF16)

        def col(name, lo=0, n=None):
            at, w = COL[name]
            return tab[:, at + lo:at + lo + (w if n is None else n)]

        def cvec(i, parts=P):
            at = COL["cvec"][0] + i
            return tab[0:parts, at:at + 1]

        def row(name, n=D):
            return rows[:, ROW[name]:ROW[name] + n]

        ident = col("ident")

        f0 = sb("f0", [E0 + 1, 4, B])
        oh0 = sb("oh0", [E0 + 1, 2, B])
        wsel = sb("wsel", [A, A, B])
        bias0 = sb("bias0", [A, B])
        ang = sb("ang", [P, 4, B])
        silu_t = sb("silu_t", [P, B])
        emb = sb("emb", [B, 2 * D])
        f2 = sb("f2", [E2, 4, B])
        eidx = sb("eidx", [1, B], I32)
        oh2 = sb("oh2", [E2, B])
        bi_sel = sb("bi_sel", [P, C, B])
        eps = sb("eps", [P, 2])

        x_in = sb("x_in", [P, NT, D])
        res = sb("res", [P, NT, D])
        resb = sb("resb", [P, NT, D])
        nrm = sb("nrm", [P, NT, D])
        hid = nrm[0:A]
        hid2 = resb[0:A + 1]
        xt = sb("xt", [P, NT, P])
        fm = sb("fm", [P, SLOTS, H, S])
        bn = sb("bn", [P, NT, 6])
        mv = sb("mv", [P, NT, 2])
        lnv = sb("lnv", [P, NT])
        rstd = sb("rstd", [P, NT])
        mx = sb("mx", [P, NT, H])
        rsum = sb("rsum", [P, NT, H])
        selv = sb("selv", [P, NT, 3 * D])
        adav = sb("adav", [P, SLOTS, 2 * D])
        qkv = sb("qkv", [P, SLOTS, 3 * D])
        qkt = sb("qkt", [P, SLOTS, 2, HG, S])
        qbd = sb("qbd", [P, SLOTS, HG, NB, S])
        kex = sb("kex", [P, SLOTS, HG, H4, S])
        vbd = sb("vbd", [P, SLOTS, NB, HG, VW])
        sc = sb("sc", [P, SLOTS, H, S])
        vrep = sb("vrep", [P, SLOTS, NB, D])
        pt = sb("pt", [P, SLOTS, HG, P])
        cx = sb("cx", [P, SLOTS, D])
        cxt = sb("cxt", [P, SLOTS, P])
        hg = sb("hg", [P, SLOTS, C, P])
        experts0 = hg[0:E0 + 1].rearrange("p k c q -> p (k c q)")[:, 0:A * A + 2 * A]
        evec2 = sc[0:E2, 0].rearrange("p h s -> p (h s)")
        ada_b = cx[0:B, 0:2].rearrange("p k q -> p (k q)")
        wexp = sb("wexp", [P, W_SLOTS, NB, 2 * FF])

        done = {name: sem("done_" + name) for name in STEP if STEP[name][0] != "sp"}
        loaded = {n: sem("loaded_" + n) for n in
                  ("xt", "x", "cvec", "tab0", "tab_ada", "tab1", "tab3", "rows", "experts0", "idx0", "idx1",
                  "idx2", "up33", "ada_b", "evec2",
                   "gate", "mask")}
        landed = {n: [sem(f"landed_{n}_{k}") for k in range(SLOTS)] for n in TRANSFERS}
        wl_landed = [sem("wl_even_landed"), sem("wl_odd_landed")]
        idle_ready = sem("idle_ready")
        preset = sem("preset")
        dchain = sem("dve_chain")
        achain = sem("act_chain")
        pchain = sem("pool_chain")
        stored = sem("stored")

        def arrived(eng, name, t):
            if name.startswith("wl"):
                piece = t * NB + int(name[-1])
                eng.wait_ge(wl_landed[piece % 2], 32 * (piece // 2 + 1))
                return
            eng.wait_ge(landed[name][t % SLOTS], 16 * TRANSFERS[name] * (t // SLOTS + 1))

        def scores(name, t):
            return bank[BANK_OF[name, t]][:].rearrange("p (h s) -> p h s", h=H)

        def reuse(eng, name, t):
            for reader, rt in PREVIOUS[name, t]:
                if STEP[reader][0] == "sp":
                    arrived(eng, reader, rt)
                else:
                    eng.wait_ge(done[reader], rt + 1)

        block = ctx.enter_context(nc.Block())

        @block.sync
        def _(sp):
            t1 = COL["wqkv1"][0]
            t3 = COL["wqkv3"][0]
            at = COL["cvec"][0]
            sp.dma_start(tab[:, at:at + 32], a["tab"][:, at:at + 32]).then_inc(loaded["cvec"], 16)
            sp.dma_start(experts0, a["experts0"]).then_inc(loaded["experts0"], 16)
            sp.dma_start(xt[:].rearrange("p t s -> p (t s)"), a["xt"]).then_inc(loaded["xt"], 16)
            sp.dma_start(tab[:, 0:at], a["tab"][:, 0:at]).then_inc(loaded["tab0"], 16)
            sp.dma_start(tab[:, at + 32:t1], a["tab"][:, at + 32:t1]).then_inc(loaded["tab_ada"], 16)
            sp.dma_start(x_in[:], a["x"].rearrange("t p d -> p t d")).then_inc(loaded["x"], 16)
            sp.dma_start(evec2, a["evec2"]).then_inc(loaded["evec2"], 16)
            sp.dma_start(rows[:], bass.AP(a["rows"].tensor, 0, [[0, P], [1, NROW]])).then_inc(loaded["rows"], 16)
            sp.dma_start(mask_u8[:], a["mask"]).then_inc(loaded["mask"], 16)
            sp.dma_start(tab[:, t1:t3], a["tab"][:, t1:t3]).then_inc(loaded["tab1"], 16)
            sp.dma_start(gate[:], a["gate"]).then_inc(loaded["gate"], 16)
            sp.dma_start(tab[:, t3:NCOL], a["tab"][:, t3:NCOL]).then_inc(loaded["tab3"], 16)
            for name, engine, t in ORDER:
                if engine != "sp":
                    continue
                k = t % SLOTS
                layer = name[-1]
                if name != "store":
                    reuse(sp, name, t)
                    sig = landed[name][k] if name in landed else wl_landed[int(name[-1]) % 2]
                if name == "ada":
                    if t == 0:
                        sp.wait_ge(done["w_embc"], 1)
                    for_tokens = emb[t * NB:(t + 1) * NB, None, :].broadcast_to([NB, S, 2 * D])
                    sp.dma_start(adav[:, k, :], for_tokens).then_inc(sig, 16)
                elif name == "fs":
                    sp.dma_start(fm[:, k].rearrange("p h k -> p (h k)"), a["fside"][t]).then_inc(sig, 16)
                elif name in ("wl0", "wl1", "wl2", "wl3"):
                    b = int(name[-1])
                    if t == 0 and b < 2:
                        sp.wait_ge(done["w_oh2"], 1)
                    if b > 1:
                        arrived(sp, f"wl{b - 2}", t)
                    elif t > 0:
                        arrived(sp, f"wl{b + 2}", t - 1)
                    e = sp.value_load(eidx[0:1, t * NB + b:t * NB + b + 1], min_val=0, max_val=E2 - 1)
                    sp.dma_start(wexp[:, t % W_SLOTS, b, :],
                                 a["wexp"][bass.ds(e, 1), :, :].rearrange("o p n -> (o p) n")).then_inc(sig, 16)
                    sp.dma_start(selv[b * S:(b + 1) * S, t, :],
                                 a["eout2"][bass.ds(e, 1), :].broadcast_to([S, 3 * D])).then_inc(sig, 16)
                elif name in ("vw1", "vw3"):
                    sp.wait_ge(done["qkvb" + layer], t + 1)
                    sp.dma_start(vdram[k], qkv[:, k, 2 * D:3 * D]).then_inc(sig, 16)
                elif name in ("vr1", "vr3"):
                    arrived(sp, "vw" + layer, t)
                    for h in range(H4):
                        sp.dma_start(vrep[h * S:(h + 1) * S, k],
                                     vdram[k].rearrange("(b s) d -> s b d", b=NB)).then_inc(sig, 16)
                elif name == "store":
                    sp.wait_ge(done["gate"], t + 1)
                    sp.dma_start(out[t], nrm[:, t, :]).then_inc(stored, 16)
            sp.wait_ge(stored, 16 * NT)

        @block.tensor
        def _(pe):
            pe.wait_ge(idle_ready, 1)
            for _ in range(WARM_UP):
                pe.matmul(bank[BANK_ONCE][:, 0:P], idle_bf[:], idle_bf[:], start=True, stop=True)

            def transpose(dst, src):
                return pe.transpose(dst, src, ident)

            for name, engine, t in ORDER:
                if engine != "pe":
                    continue
                k = t % SLOTS
                ps = bank[BANK_OF[name, t]] if name not in ONCE else bank[BANK_ONCE]
                reuse(pe, name, t)
                layer = name[-1]
                if name == "w_sel":
                    pe.wait_ge(loaded["experts0"], 16)
                    pe.wait_ge(done["w_oh0"], 1)
                    for n in range(2):
                        pe.matmul(bank[BANK_SEL[n]][0:B, :], oh0[:, 0, :], experts0[:, n * 512:(n + 1) * 512],
                                  start=True, stop=True)
                    pe.matmul(ps[0:A, 0:B], experts0[:, A * A:A * A + A], oh0[:, 0, :], start=True, stop=False)
                    mm = pe.matmul(ps[0:A, 0:B], experts0[:, A * A + A:A * A + 2 * A], oh0[:, 1, :],
                                   start=False, stop=True)
                elif name == "w_emb":
                    pe.wait_ge(done["w_silu"], 1)
                    pe.wait_ge(done["w_selc"], 1)
                    pe.wait_ge(loaded["tab_ada"], 16)
                    mm = pe.matmul(ps[0:B, 0:2 * D], silu_t[:], col("w_ada"), start=True, stop=True)
                elif name == "w_bi":
                    pe.wait_ge(done["w_oh2"], 1)
                    pe.wait_ge(done["w_embc"], 1)
                    pe.wait_ge(loaded["evec2"], 16)
                    for c in range(C):
                        mm = pe.matmul(ps[:, c * B:(c + 1) * B], evec2[:, c * P:(c + 1) * P], oh2[:],
                                       start=True, stop=True)
                elif name == "down":
                    if t == 0:
                        pe.wait_ge(loaded["tab0"], 16)
                        pe.wait_ge(loaded["xt"], 16)
                    mm = pe.matmul(ps[0:A, 0:P], col("down_wt"), xt[:, t, :], start=True, stop=True)
                elif name == "expert":
                    pe.wait_ge(done["gelu0"], t + 1)
                    if t == 0:
                        pe.wait_ge(done["w_selc"], 1)
                    for b in range(NB):
                        mm = pe.matmul(ps[0:A, b * S:(b + 1) * S], wsel[:, :, t * NB + b],
                                       hid[:, t, b * S:(b + 1) * S], start=True, stop=True)
                elif name == "up":
                    pe.wait_ge(done["ebias"], t + 1)
                    if t == 0:
                        pe.wait_ge(loaded["up33"], 16)
                        pe.wait_ge(preset, PRESETS)
                    mm = pe.matmul(ps[:, 0:D], hid2[:, t, :], up33[:], start=True, stop=True)
                elif name in ("tr_b", "tr_d"):
                    pe.wait_ge(done["aff_b" if name == "tr_b" else "res2"], t + 1)
                    mm = transpose(ps[:, 0:P], res[:, t, :])
                elif name in ("tr_c", "tr_f", "tr_g"):
                    pe.wait_ge(done["norm_" + layer], t + 1)
                    mm = transpose(ps[:, 0:P], nrm[:, t, :])
                elif name in ("qkv1", "qkv3"):
                    if t == 0:
                        pe.wait_ge(loaded["tab" + layer], 16)
                    pe.wait_ge(done["ev_b" if layer == "1" else "ev_f"], t + 1)
                    mm = pe.matmul(ps[:, 0:3 * D], xt[:, t, :], col("wqkv" + layer), start=True, stop=True)
                elif name in ("sc1", "sc3"):
                    pe.wait_ge(done["qbd" + layer], t + 1)
                    pe.wait_ge(done["kex" + layer], t + 1)
                    if t == 0:
                        pe.wait_ge(done["w_neg"], 1)
                    masked = mask_neg[:, t, :] if layer == "1" else causal_neg[:]
                    pe.matmul(ps[:].rearrange("p (h s) -> p h s", h=H), ident_bf[:],
                              masked[:, None, :].broadcast_to([P, H, S]), start=True, stop=False)
                    for g in range(HG):
                        mm = pe.matmul(ps[:, g * P:(g + 1) * P], qbd[:, k, g].rearrange("p b s -> p (b s)"),
                                       kex[:, k, g].rearrange("p h s -> p (h s)"), start=False, stop=(g == HG - 1))
                elif name in ("pt1", "pt3"):
                    pe.wait_ge(done["exp" + layer], t + 1)
                    for g in range(HG):
                        mm = transpose(ps[:, g * P:(g + 1) * P],
                                       sc[:, k, g * H4:(g + 1) * H4, :].rearrange("p h s -> p (h s)"))
                elif name in ("ctx1", "ctx3"):
                    pe.wait_ge(done["evpt" + layer], t + 1)
                    pe.wait_ge(done["vbd" + layer], t + 1)
                    if t == 0:
                        pe.wait_ge(done["w_pre"], 1)
                    for g in range(HG):
                        for b in range(NB):
                            mm = pe.matmul(ps[b * S:(b + 1) * S, g * VW:(g + 1) * VW],
                                           pt[:, k, g, b * S:(b + 1) * S], vbd[:, k, b, g, :], start=True, stop=True,
                                           tile_position=(0, b * S))
                elif name in ("ct1", "ct3"):
                    pe.wait_ge(done["cn" + layer], t + 1)
                    mm = transpose(ps[:, 0:P], cx[:, k, :])
                elif name in ("wo1", "wo3"):
                    pe.wait_ge(done["evct" + layer], t + 1)
                    mm = pe.matmul(ps[:, 0:D], cxt[:, k, :], col("wo" + layer), start=True, stop=True)
                elif name in ("ff1", "ff3"):
                    pe.wait_ge(done["ev_c" if layer == "1" else "ev_g"], t + 1)
                    for c in range(C):
                        mm = pe.matmul(ps[:, c * P:(c + 1) * P], col("w1" + layer, c * P, P), xt[:, t, :],
                                       start=True, stop=True)
                elif name in ("fo1", "fo3"):
                    pe.wait_ge(done["act" + layer], t + 1)
                    for c in range(C):
                        mm = pe.matmul(ps[:, 0:D], hg[:, k, c, :], col("w2" + layer, c * D, D),
                                       start=(c == 0), stop=(c == C - 1))
                elif name == "e1":
                    pe.wait_ge(done["ev_d"], t + 1)
                    arrived(pe, "wl2", t)
                    arrived(pe, "wl3", t)
                    for b in range(NB):
                        mm = pe.matmul(ps[b * S:(b + 1) * S, :], xt[:, t, b * S:(b + 1) * S],
                                       wexp[:, t % W_SLOTS, b, 0:FF], start=True, stop=True, tile_position=(0, b * S))
                elif name == "et":
                    pe.wait_ge(done["eve1"], t + 1)
                    for c in range(C):
                        mm = transpose(ps[:, c * P:(c + 1) * P], pt[:, k, c, :])
                elif name == "e2":
                    pe.wait_ge(done["gelu2"], t + 1)
                    for c in range(C):
                        for b in range(NB):
                            mm = pe.matmul(ps[b * S:(b + 1) * S, 0:D], hg[:, k, c, b * S:(b + 1) * S],
                                           wexp[:, t % W_SLOTS, b, FF + c * D:FF + (c + 1) * D],
                                           start=(c == 0), stop=(c == C - 1), tile_position=(0, b * S))
                mm.then_inc(done[name], 1)

        @block.scalar
        def _(act):
            chain = [0]

            def link(ins):
                chain[0] += 1
                ins.then_inc(achain, 1)
                act.wait_ge(achain, chain[0])

            def spread(name, parts, n):
                return bass.AP(a[name].tensor, 0, [[0, parts], [1, n]])

            act.dma_start(idx0[:], spread("idx0", E0 + 1, B)).then_inc(loaded["idx0"], 16)
            act.dma_start(idx1[:], spread("idx1", P, B)).then_inc(loaded["idx1"], 16)
            act.dma_start(idx2[:], spread("idx2", E2, B)).then_inc(loaded["idx2"], 16)
            act.dma_start(up33[:], a["up33"]).then_inc(loaded["up33"], 16)
            act.dma_start(ada_b, spread("ada_b", B, 2 * D)).then_inc(loaded["ada_b"], 16)
            table = ["none"]
            for name, engine, t in ORDER:
                if engine != "act":
                    continue
                k = t % SLOTS
                layer = name[-1]
                reuse(act, name, t)
                if name == "w_silu":
                    act.wait_ge(done["w_ang"], 1)
                    link(act.activation(silu_t[:], ang[:, 0, :], ACT.Sin))
                    ins = act.activation(silu_t[:], silu_t[:], ACT.Silu)
                    table[0] = "silu"
                elif name == "gelu0":
                    act.wait_ge(done["down"], t + 1)
                    if t == 0:
                        act.wait_ge(loaded["cvec"], 16)
                    table[0] = "gelu"
                    ins = act.activation(hid[:, t, :], bank[BANK_OF["down", t]][0:A, 0:P], ACT.Gelu, bias=cvec(C_DOWN_B, A))
                elif name.startswith("rstd"):
                    act.wait_ge(done["stat_" + layer], t + 1)
                    if t == 0:
                        act.wait_ge(preset, PRESETS)
                    if table[0] != "ln":
                        act.preload_act_table_set("natural_log_exp_and_others")
                        table[0] = "ln"
                    link(act.activation(lnv[:, t:t + 1], mv[:, t, 1:2], ACT.Ln,
                                        bias=eps[:, 1:2] if layer == "e" else eps[:, 0:1]))
                    ins = act.activation(rstd[:, t:t + 1], lnv[:, t:t + 1], ACT.Exp, scale=-0.5)
                elif name in ("ev_b", "ev_d"):
                    act.wait_ge(done["tr_" + layer], t + 1)
                    ins = act.activation(xt[:, t, :], bank[BANK_OF["tr_" + layer, t]][:, 0:P], ACT.Copy)
                elif name in ("exp1", "exp3"):
                    act.wait_ge(done["sub" + layer], t + 1)
                    if table[0] != "ln":
                        act.preload_act_table_set("natural_log_exp_and_others")
                        table[0] = "ln"
                    ins = act.activation(sc[:, k], sc[:, k], ACT.Exp)
                elif name in ("evpt1", "evpt3"):
                    act.wait_ge(done["pt" + layer], t + 1)
                    ins = act.activation(pt[:, k].rearrange("p c q -> p (c q)"), bank[BANK_OF["pt" + layer, t]][:], ACT.Copy)
                elif name in ("evct1", "evct3"):
                    act.wait_ge(done["ct" + layer], t + 1)
                    ins = act.activation(cxt[:, k, :], bank[BANK_OF["ct" + layer, t]][:, 0:P], ACT.Copy)
                elif name in ("act1", "act3"):
                    act.wait_ge(done["ff" + layer], t + 1)
                    table[0] = "gelu"
                    for c in range(C):
                        ins = act.activation(hg[:, k, c, :], bank[BANK_OF["ff" + layer, t]][:, c * P:(c + 1) * P],
                                             ACT.Gelu_apprx_sigmoid if layer == "1" else ACT.Gelu,
                                             bias=cvec((C_B1_1 if layer == "1" else C_B1_3) + c))
                elif name == "gelu2":
                    act.wait_ge(done["eb"], t + 1)
                    table[0] = "gelu"
                    ins = act.activation(hg[:, k], hg[:, k], ACT.Gelu)
                ins.then_inc(done[name], 1)

        @block.vector
        def _(dve):
            chain = [0]

            def link(ins):
                chain[0] += 1
                ins.then_inc(dchain, 1)
                dve.wait_ge(dchain, chain[0])

            dve.memset(hid2[A:A + 1, :, :], 1.0).then_inc(preset, 1)
            dve.memset(eps[:, 0:1], EPS).then_inc(preset, 1)
            dve.memset(eps[:, 1:2], EPS2).then_inc(preset, 1)
            def stream(norm, t):
                return x_in[:, t, :] if norm == "f" else res[:, t, :]

            prev_norm = {"a": "res0", "b": "aff_a", "c": "res1", "e": "res3", "f": "aff_e", "g": "res4"}
            for name, engine, t in ORDER:
                if engine != "dve":
                    continue
                k = t % SLOTS
                layer = name[-1]
                reuse(dve, name, t)
                if name == "w_oh0":
                    dve.wait_ge(loaded["idx0"], 16)
                    dve.wait_ge(loaded["cvec"], 16)
                    link(dve.tensor_copy(f0[:, 0, :], idx0[:]))
                    link(dve.tensor_scalar(f0[:, 1, :], f0[:, 0, :], 0.0, float(E0 - 1), ALU.max, ALU.min))
                    link(dve.tensor_tensor(f0[:, 2, :], f0[:, 0, :], f0[:, 1, :], ALU.not_equal))
                    link(dve.tensor_scalar(f0[:, 3, :], f0[:, 2, :], float(E0 + 1), None, ALU.mult))
                    link(dve.tensor_tensor(f0[:, 2, :], f0[:, 1, :], f0[:, 3, :], ALU.add))
                    link(dve.tensor_scalar(f0[:, 3, :], f0[:, 2, :], float(E0), None, ALU.min))
                    dve.tensor_scalar(oh0[:, 0, :], f0[:, 3, :], cvec(C_IOTA, E0 + 1), None, ALU.is_equal)
                    ins = dve.tensor_scalar(oh0[:, 1, :], f0[:, 1, :], cvec(C_IOTA, E0 + 1), None, ALU.is_equal)
                elif name == "w_ang":
                    dve.wait_ge(loaded["idx1"], 16)
                    dve.wait_ge(loaded["cvec"], 16)
                    link(dve.tensor_copy(ang[:, 0, :], idx1[:]))
                    link(dve.tensor_scalar(ang[:, 1, :], ang[:, 0, :], 40.0, cvec(C_FREQ), ALU.mult, ALU.mult))
                    link(dve.tensor_scalar(ang[:, 2, :], ang[:, 1, :], cvec(C_PHASE), 1.0 / TWO_PI, ALU.add, ALU.mult))
                    link(dve.tensor_scalar(ang[:, 3, :], ang[:, 2, :], ROUND, ROUND, ALU.add, ALU.subtract))
                    link(dve.scalar_tensor_tensor(ang[:, 0, :], ang[:, 3, :], -PI_A, ang[:, 1, :], ALU.mult, ALU.add))
                    link(dve.scalar_tensor_tensor(ang[:, 1, :], ang[:, 3, :], -PI_B, ang[:, 0, :], ALU.mult, ALU.add))
                    link(dve.scalar_tensor_tensor(ang[:, 2, :], ang[:, 3, :], -PI_C, ang[:, 1, :], ALU.mult, ALU.add))
                    link(dve.tensor_scalar(ang[:, 1, :], ang[:, 2, :], cvec(C_PHASE), 3.1415925, ALU.add, ALU.min))
                    ins = dve.tensor_scalar(ang[:, 0, :], ang[:, 1, :], -3.1415925, None, ALU.max)
                elif name == "w_oh2":
                    dve.wait_ge(loaded["idx2"], 16)
                    dve.wait_ge(loaded["cvec"], 16)
                    link(dve.tensor_copy(f2[:, 0, :], idx2[:]))
                    link(dve.tensor_scalar(f2[:, 1, :], f2[:, 0, :], 0.0, float(E2), ALU.is_lt, ALU.mult))
                    link(dve.tensor_tensor(f2[:, 2, :], f2[:, 0, :], f2[:, 1, :], ALU.add))
                    link(dve.tensor_scalar(f2[:, 3, :], f2[:, 2, :], 0.0, float(E2 - 1), ALU.max, ALU.min))
                    dve.tensor_scalar(oh2[:], f2[:, 3, :], cvec(C_IOTA, E2), None, ALU.is_equal)
                    ins = dve.tensor_copy(eidx[:], f2[0:1, 3, :])
                elif name == "w_selc":
                    dve.wait_ge(done["w_sel"], 1)
                    for n in range(2):
                        dve.transpose(wsel[:, 16 * n:16 * n + 16, :].rearrange("a o b -> a (o b)"),
                                      bank[BANK_SEL[n]][0:B, :])
                    ins = dve.tensor_copy(bias0[:], bank[BANK_ONCE][0:A, 0:B])
                elif name == "w_embc":
                    dve.wait_ge(done["w_emb"], 1)
                    dve.wait_ge(loaded["ada_b"], 16)
                    link(dve.tensor_tensor(emb[:], bank[BANK_ONCE][0:B, 0:2 * D], ada_b, ALU.add))
                    ins = dve.tensor_scalar(emb[:, 0:D], emb[:, 0:D], 1.0, None, ALU.add)
                elif name == "w_bic":
                    dve.wait_ge(done["w_bi"], 1)
                    ins = dve.tensor_copy(bi_sel[:].rearrange("p c b -> p (c b)"), bank[BANK_ONCE][:, 0:C * B])
                elif name == "ebias":
                    dve.wait_ge(done["expert"], t + 1)
                    if t == 0:
                        dve.wait_ge(done["w_selc"], 1)
                    ins = dve.tensor_tensor(
                        hid2[0:A, t, :].rearrange("o (b s) -> o b s", b=NB),
                        bank[BANK_OF["expert", t]][0:A, 0:P].rearrange("o (b s) -> o b s", b=NB),
                        bias0[:, t * NB:(t + 1) * NB, None].broadcast_to([A, NB, S]), ALU.add)
                elif name == "res0":
                    dve.wait_ge(done["up"], t + 1)
                    if t == 0:
                        dve.wait_ge(loaded["x"], 16)
                    ins = dve.tensor_tensor(res[:, t, :], bank[BANK_OF["up", t]][:, 0:D], x_in[:, t, :], ALU.add)
                elif name.startswith("stat"):
                    dve.wait_ge(done[prev_norm[layer]], t + 1)
                    link(dve.bn_stats(bn[:, t, :], stream(layer, t)))
                    ins = dve.bn_aggr(mv[:, t, :], bn[:, t, :])
                elif name in ("ev_c", "ev_f", "ev_g"):
                    dve.wait_ge(done["tr_" + layer], t + 1)
                    scale, shift = {"c": (C_G2, C_BETA2), "f": (C_G31, C_B31), "g": (C_G32, C_B32)}[layer]
                    ins = dve.tensor_scalar(xt[:, t, :], bank[BANK_OF["tr_" + layer, t]][:, 0:P], cvec(scale),
                                            cvec(shift), ALU.mult, ALU.add)
                elif name.startswith("norm"):
                    dve.wait_ge(done["rstd_" + layer], t + 1)
                    ins = dve.tensor_scalar(nrm[:, t, :], stream(layer, t), mv[:, t, 0:1], rstd[:, t:t + 1],
                                            ALU.subtract, ALU.mult)
                elif name == "aff_b":
                    dve.wait_ge(done["norm_b"], t + 1)
                    arrived(dve, "ada", t)
                    link(dve.tensor_tensor(res[:, t, :], nrm[:, t, :], adav[:, k, 0:D], ALU.mult))
                    ins = dve.tensor_tensor(res[:, t, :], res[:, t, :], adav[:, k, D:2 * D], ALU.add)
                elif name in ("qkvb1", "qkvb3"):
                    dve.wait_ge(done["qkv" + layer], t + 1)
                    if t == 0:
                        dve.wait_ge(loaded["rows"], 16)
                    ins = dve.tensor_tensor(qkv[:, k, :], bank[BANK_OF["qkv" + layer, t]][:, 0:3 * D],
                                            row("bqkv" + layer, 3 * D), ALU.add)
                elif name in ("qkt1", "qkt3"):
                    dve.wait_ge(done["qkvb" + layer], t + 1)
                    ins = dve.transpose(qkt[:, k].rearrange("p j g s -> p (j g s)"), qkv[:, k, 0:2 * D])
                elif name == "kex3":
                    if t == 0:
                        dve.wait_ge(loaded["tab0"], 16)
                    dve.wait_ge(done["qkt3"], t + 1)
                    ins = dve.tensor_tensor(kex[:, k], qkt[:, k, 1, :, None, :].broadcast_to([P, HG, H4, S]),
                                            col("head_mask")[:, None, :, None].broadcast_to([P, HG, H4, S]), ALU.mult)
                elif name == "sub3":
                    dve.wait_ge(done["mx3"], t + 1)
                    ins = dve.tensor_tensor(sc[:, k], scores("sc3", t), mx[:, t, :, None].broadcast_to([P, H, S]),
                                            ALU.subtract)
                elif name == "sb1":
                    dve.wait_ge(done["sc1"], t + 1)
                    arrived(dve, "fs", t)
                    ins = dve.tensor_tensor(sc[:, k], scores("sc1", t), fm[:, k], ALU.add)
                elif name in ("mx1", "mx3"):
                    dve.wait_ge(done["sb1" if layer == "1" else "sc3"], t + 1)
                    ins = dve.tensor_reduce(mx[:, t, :], sc[:, k] if layer == "1" else scores("sc3", t), AX.X, ALU.max)
                elif name in ("cn1", "cn3"):
                    dve.wait_ge(done["ctx" + layer], t + 1)
                    p4 = bank[BANK_OF["ctx" + layer, t]][:, 0:HG * VW].rearrange("p (g w) -> p g w", g=HG)
                    link(dve.reciprocal(rsum[:, t, :].rearrange("p (g h) -> p g h", g=HG), p4[:, :, H4 * DH:VW]))
                    ins = dve.tensor_tensor(
                        cx[:, k, :].rearrange("p (g h d) -> p g h d", g=HG, h=H4),
                        p4[:, :, 0:H4 * DH].rearrange("p g (h d) -> p g h d", h=H4),
                        rsum[:, t, :].rearrange("p (g h) -> p g h", g=HG)[:, :, :, None].broadcast_to(
                            [P, HG, H4, DH]), ALU.mult)
                elif name in ("res1", "res4"):
                    l_ = "1" if name == "res1" else "3"
                    dve.wait_ge(done["wo" + l_], t + 1)
                    dve.wait_ge(done["xbo" + l_], t + 1)
                    ins = dve.tensor_tensor(res[:, t, :], bank[BANK_OF["wo" + l_, t]][:, 0:D],
                                            resb[:, t, :], ALU.add)
                elif name == "res2":
                    dve.wait_ge(done["fo1"], t + 1)
                    dve.wait_ge(done["xb21"], t + 1)
                    ins = dve.tensor_tensor(res[:, t, :], bank[BANK_OF["fo1", t]][:, 0:D], resb[:, t, :], ALU.add)
                elif name == "eve1":
                    dve.wait_ge(done["e1"], t + 1)
                    ins = dve.tensor_copy(pt[:, k].rearrange("p c q -> p (c q)"), bank[BANK_OF["e1", t]][:])
                elif name == "eb":
                    dve.wait_ge(done["et"], t + 1)
                    if t == 0:
                        dve.wait_ge(done["w_bic"], 1)
                    ins = dve.tensor_tensor(
                        hg[:, k].rearrange("p c (b s) -> p c b s", b=NB),
                        bank[BANK_OF["et", t]][:].rearrange("p (c b s) -> p c b s", c=C, b=NB),
                        bi_sel[:, :, t * NB:(t + 1) * NB, None].broadcast_to([P, C, NB, S]), ALU.add)
                elif name == "res3":
                    dve.wait_ge(done["e2"], t + 1)
                    dve.wait_ge(done["xbo2"], t + 1)
                    ins = dve.tensor_tensor(res[:, t, :], bank[BANK_OF["e2", t]][:, 0:D], resb[:, t, :], ALU.add)
                elif name == "res5":
                    dve.wait_ge(done["fo3"], t + 1)
                    dve.wait_ge(done["xb23"], t + 1)
                    ins = dve.tensor_tensor(resb[:, t, :], bank[BANK_OF["fo3", t]][:, 0:D], resb[:, t, :], ALU.add)
                elif name == "gate":
                    if t == 0:
                        dve.wait_ge(loaded["gate"], 16)
                    dve.wait_ge(done["res5"], t + 1)
                    ins = dve.scalar_tensor_tensor(nrm[:, t, :], resb[:, t, :], gate[:, t:t + 1], x_in[:, t, :],
                                                   ALU.mult, ALU.add)
                ins.then_inc(done[name], 1)

        @block.gpsimd
        def _(pool):
            chain = [0]

            def link(ins):
                chain[0] += 1
                ins.then_inc(pchain, 1)
                pool.wait_ge(pchain, chain[0])

            pool.memset(idle_bf[:], 0.0).then_inc(idle_ready, 1)
            for name, engine, t in ORDER:
                if engine != "pool":
                    continue
                k = t % SLOTS
                layer = name[-1]
                reuse(pool, name, t)
                if name == "w_pre":
                    pool.wait_ge(loaded["tab0"], 16)
                    ins = pool.tensor_copy(
                        vbd[:].rearrange("p k b g w -> p (k b g) w")[:, :, H4 * DH:VW],
                        col("seq_mask")[:, None, :].broadcast_to([P, SLOTS * NB * HG, H4]))
                elif name == "w_neg":
                    pool.wait_ge(loaded["tab0"], 16)
                    pool.tensor_copy(ident_bf[:], ident)
                    pool.wait_ge(loaded["tab_ada"], 16)
                    pool.tensor_copy(causal_neg[:], col("causal"))
                    pool.wait_ge(loaded["mask"], 16)
                    ins = pool.tensor_scalar(mask_neg[:].rearrange("p t k -> p (t k)"), mask_u8[:], NEG, None,
                                             ALU.mult)
                elif name == "aff_a":
                    pool.wait_ge(done["norm_a"], t + 1)
                    if t == 0:
                        pool.wait_ge(loaded["rows"], 16)
                    link(pool.tensor_tensor(res[:, t, :], nrm[:, t, :], row("g0"), ALU.mult))
                    ins = pool.tensor_tensor(res[:, t, :], res[:, t, :], row("be0"), ALU.add)
                elif name == "aff_e":
                    pool.wait_ge(done["norm_e"], t + 1)
                    link(pool.tensor_tensor(res[:, t, :], nrm[:, t, :], selv[:, t, D:2 * D], ALU.mult))
                    ins = pool.tensor_tensor(x_in[:, t, :], res[:, t, :], selv[:, t, 2 * D:3 * D], ALU.add)
                elif name in ("xbo1", "xbo3"):
                    pool.wait_ge(done["aff_b" if layer == "1" else "aff_e"], t + 1)
                    before = res if layer == "1" else x_in
                    ins = pool.tensor_tensor(resb[:, t, :], before[:, t, :], row("bo" + layer), ALU.add)
                elif name == "kex1":
                    if t == 0:
                        pool.wait_ge(loaded["tab0"], 16)
                    pool.wait_ge(done["qkt1"], t + 1)
                    ins = pool.tensor_tensor(kex[:, k], qkt[:, k, 1, :, None, :].broadcast_to([P, HG, H4, S]),
                                            col("head_mask")[:, None, :, None].broadcast_to([P, HG, H4, S]), ALU.mult)
                elif name in ("qbd1", "qbd3"):
                    pool.wait_ge(done["qkt" + layer], t + 1)
                    at = COL["cvec"][0] + 20
                    ins = pool.tensor_tensor(qbd[:, k], qkt[:, k, 0, :, None, :].broadcast_to([P, HG, NB, S]),
                                             tab[:, None, at:at + NB, None].broadcast_to([P, HG, NB, S]), ALU.mult)
                elif name in ("vbd1", "vbd3"):
                    arrived(pool, "vr" + layer, t)
                    if t == 0:
                        pool.wait_ge(loaded["tab0"], 16)
                    n = NB * HG
                    ins = pool.tensor_tensor(
                        vbd[:, k].rearrange("p b g w -> p (b g) w")[:, :, 0:H4 * DH].rearrange(
                            "p n (h d) -> p n h d", h=H4),
                        vrep[:, k].rearrange("p b (g h d) -> p (b g) h d", g=HG, h=H4),
                        col("seq_mask")[:, None, :, None].broadcast_to([P, n, H4, DH]), ALU.mult)
                elif name == "sub1":
                    pool.wait_ge(done["mx1"], t + 1)
                    ins = pool.tensor_tensor(sc[:, k], sc[:, k], mx[:, t, :, None].broadcast_to([P, H, S]),
                                             ALU.subtract)
                elif name == "xb21":
                    pool.wait_ge(done["res1"], t + 1)
                    ins = pool.tensor_tensor(resb[:, t, :], res[:, t, :], row("b21"), ALU.add)
                elif name == "xbo2":
                    pool.wait_ge(done["res2"], t + 1)
                    arrived(pool, "wl2", t)
                    arrived(pool, "wl3", t)
                    ins = pool.tensor_tensor(resb[:, t, :], res[:, t, :], selv[:, t, 0:D], ALU.add)
                elif name == "xb23":
                    pool.wait_ge(done["res4"], t + 1)
                    link(pool.tensor_tensor(resb[:, t, :], res[:, t, :], row("b23"), ALU.add))
                    ins = pool.tensor_tensor(resb[:, t, :], resb[:, t, :], x_in[:, t, :], ALU.subtract)
                ins.then_inc(done[name], 1)


def kernel(**inputs):
    import numpy as np
    import concourse.bacc as _bacc
    from concourse import mybir as _mybir
    from concourse.bass_utils import run_bass_kernel_spmd as _run

    v = {n: np.asarray(a) for n, a in inputs.items()}
    f = np.float32

    def cols(a):
        return np.ascontiguousarray(a.reshape(-1, P).T)

    def chunks(w):
        return w.reshape(C, P, -1).transpose(1, 0, 2).reshape(P, -1)

    p = np.arange(P)
    cvec = np.zeros((P, 32), f)
    cvec[0:A, C_DOWN_B] = v["L0_cond_down_b"]
    half = D // 2
    freqs = np.exp(np.arange(half, dtype=f) * f(-math.log(10000.0) / (half - 1))).astype(f)
    cvec[:, C_FREQ] = np.concatenate([freqs, freqs])
    cvec[half:, C_PHASE] = math.pi / 2
    cvec[:, C_IOTA] = p
    for i, n in ((C_BV1, "L1_cond_bv"), (C_G2, "L1_cond_g2"), (C_BETA2, "L1_cond_beta2"), (C_BV3, "L3_cond_bv"),
                 (C_G31, "L3_cond_gamma1"), (C_B31, "L3_cond_beta1"), (C_G32, "L3_cond_gamma2"),
                 (C_B32, "L3_cond_beta2")):
        cvec[:, i] = v[n]
    cvec[:, C_B1_1:C_B1_1 + C] = cols(v["L1_cond_b1"])
    cvec[:, C_B1_3:C_B1_3 + C] = cols(v["L3_cond_b1"])
    seq_mask = (p[:, None] // S == np.arange(NB)[None, :]).astype(f)
    cvec[:, 20:20 + NB] = seq_mask * f(1.0 / math.sqrt(DH))
    parts = {
        "ident": np.eye(P, dtype=f), "down_wt": v["L0_cond_down_W"].T, "seq_mask": seq_mask,
        "head_mask": ((p[:, None] % S) // DH == np.arange(H4)[None, :]).astype(f), "cvec": cvec,
        "w_ada": v["L1_cond_W_ada"],
        "causal": np.where(np.arange(S)[None, :] <= (p % S)[:, None], 0.0, NEG).astype(f),
    }
    for l in "13":
        w = {n: v[f"L{l}_cond_{n}"] for n in ("Wq", "Wk", "Wv", "Wo", "W1", "W2")}
        parts.update({"wqkv" + l: np.concatenate([w["Wq"], w["Wk"], w["Wv"]], 1), "wo" + l: w["Wo"],
                      "w1" + l: w["W1"], "w2" + l: chunks(w["W2"])})
    tab = np.concatenate([parts[n] for n, _ in COLS], 1)
    rows = np.concatenate([v[n] for n in (
        "L0_cond_ln_gamma", "L0_cond_ln_beta", "L1_cond_bq", "L1_cond_bk", "L1_cond_bv", "L1_cond_bo", "L1_cond_b2",
        "L3_cond_bq", "L3_cond_bk", "L3_cond_bv", "L3_cond_bo", "L3_cond_b2")])
    experts0 = np.concatenate([
        np.concatenate([v["L0_cond_expert_W"].reshape(E0, A * A), np.eye(A, dtype=f).reshape(1, A * A)]),
        np.concatenate([np.concatenate([v["L0_cond_expert_b"], v["L0_cond_domain_emb"]], 1),
                        np.zeros((1, 2 * A), f)])], 1)
    wi = v["L2_cond_Wi"]
    wo = v["L2_cond_Wo"].reshape(E2, C, P, D).transpose(0, 2, 1, 3).reshape(E2, P, C * D)
    laid = {
        "x": v["x"].reshape(NT, P, D),
        "xt": v["x"].reshape(NT * P, D).T,
        "tab": tab, "rows": rows, "experts0": experts0,
        "up33": np.concatenate([v["L0_cond_up_W"].T, v["L0_cond_up_b"][None]]),
        "ada_b": v["L1_cond_b_ada"],
        "evec2": v["L2_cond_bi"],
        "eout2": np.concatenate([v["L2_cond_" + n] for n in ("bo", "gamma", "beta")], 1),
        "wexp": np.concatenate([wi, wo], 2),
        "fside": v["fside_Bx16xSxS_0"].reshape(NT, NB, H, S, S).transpose(0, 1, 3, 2, 4).reshape(NT, P, H * S),
        "mask": v["mask_Bx1xSxS_bk0"].reshape(NT, P, S).transpose(1, 0, 2).reshape(P, NT * S),
        "idx0": v["itok_B_0_15"], "idx1": v["itok_B_34_63"], "idx2": v["itok_B_0_7"],
        "gate": np.repeat(v["condB_gatescore"], S).reshape(NT, P).T,
    }
    nc = _bacc.Bacc("TRN2", target_bir_lowering=False, num_devices=1)
    arrays, aps = {}, {}
    for name, x in laid.items():
        x = np.ascontiguousarray(x)
        arrays[f"in_{name}"] = x
        aps[name] = nc.dram_tensor(f"in_{name}", x.shape, _mybir.dt.from_np(x.dtype), kind="ExternalInput").ap()
    out = nc.dram_tensor("out_0", (NT, P, D), _mybir.dt.float32, kind="ExternalOutput").ap()
    aps["vdram"] = nc.dram_tensor("vdram", (SLOTS, P, D), _mybir.dt.float32, kind="Internal").ap()
    build(nc, aps, out)
    r = _run(nc, [arrays], core_ids=[0])
    return r.results[0]["out_0"].reshape(B, S, D)
```
